# Optimizing a Trainium2 kernel written in Bass

```python
import numpy as np
import jax
import jax.numpy as jnp

def _softmax(x, axis=-1):
    return jax.nn.softmax(x, axis=axis)

def _gelu(x):
    return jax.nn.gelu(x, approximate=True)

def _silu(x):
    return jax.nn.silu(x)

def _sigmoid(x):
    return jax.nn.sigmoid(x)

def _layernorm(x, axis=-1, eps=1e-05):
    m = jnp.mean(x, axis=axis, keepdims=True)
    v = jnp.var(x, axis=axis, keepdims=True)
    return (x - m) / jnp.sqrt(v + eps)

def _scatter_add(tgt, idx, src, axis=0):
    return tgt.at[idx].add(src)

def _segment_sum(src, seg, n):
    return jax.ops.segment_sum(src, seg, n)
kernel_name = 'mk_decoder_postln_d1_seqx_r4_9efbc7'

def setup_inputs(seed: int=0):
    np.random.seed(seed)
    _w = jnp.asarray

    def _rec_inputs():
        import jax
        import jax.numpy as jnp
        _rk = jax.random.key(seed)
        x = -0.000125 + 0.9999 * jax.random.normal(jax.random.fold_in(_rk, 1), (16, 128, 512), jnp.float32)
        _lenS = 128 - jax.random.randint(jax.random.fold_in(_rk, 7), (16,), 0, max(1, 128 // 4) + 1, jnp.int32)
        _lenS2 = 128 - jax.random.randint(jax.random.fold_in(_rk, 8), (16,), 0, max(1, 128 // 4) + 1, jnp.int32)
        _ctx_2048P = jax.random.normal(jax.random.fold_in(_rk, 11), (16, 16, 512), jnp.float32)
        _ctx_2048c = jax.random.dirichlet(jax.random.fold_in(_rk, 511), 0.3 * jnp.ones((16,), jnp.float32), (16, 128))
        _ctx_2048t = jnp.einsum('bsk,bkd->bsd', _ctx_2048c, _ctx_2048P)
        _ctx_2048t = _ctx_2048t * jax.lax.rsqrt(jnp.mean(jnp.square(_ctx_2048t)) + 1e-12) * 0.953939
        ctx_2048 = -0.000514642 + 1.00011 * (_ctx_2048t + 0.3 * jax.random.normal(jax.random.fold_in(_rk, 611), (16, 128, 512), jnp.float32))
        _validS = jnp.arange(128)[None, :] < _lenS[:, None]
        _validS2 = jnp.arange(128)[None, :] < _lenS2[:, None]
        _causal = jnp.tril(jnp.ones((128, 128), dtype=bool))
        mask_BxS2_bk0 = jnp.logical_not(jnp.broadcast_to(_validS2[:, :], (16, 128)))
        return (x, ctx_2048, mask_BxS2_bk0)
    x, ctx_2048, mask_BxS2_bk0 = _rec_inputs()

    def _L0_attn_setup():
        import jax, jax.numpy as jnp
        import numpy as np
        DT_RANK = 128
        DIM_INNER = 512
        D_STATE = 16
        IN_FEATURES = 512

        def _scan_combine(e1, e2):
            a1, b1 = e1
            a2, b2 = e2
            return (a1 * a2, a2 * b1 + b2)
        key = jax.random.key(seed)
        ks = jax.random.split(key, 6)
        B, L = (2, 512)
        x = jax.random.normal(ks[0], (B, L, IN_FEATURES), dtype=jnp.float32)
        out_dbc = DT_RANK + 2 * D_STATE
        W_dbc = jax.random.normal(ks[1], (out_dbc, IN_FEATURES), dtype=jnp.float32) / np.sqrt(IN_FEATURES)
        b_dbc = jax.random.normal(ks[2], (out_dbc,), dtype=jnp.float32) * 0.01
        W_dt = jax.random.normal(ks[3], (DIM_INNER, DT_RANK), dtype=jnp.float32) / np.sqrt(DT_RANK)
        b_dt = jax.random.normal(ks[4], (DIM_INNER,), dtype=jnp.float32) * 0.01
        A_log = jnp.log(jnp.tile(jnp.arange(1, D_STATE + 1, dtype=jnp.float32), (DIM_INNER, 1)))
        D = jnp.ones((DIM_INNER,), dtype=jnp.float32)
        return {'x': x, 'W_dbc': W_dbc, 'b_dbc': b_dbc, 'W_dt': W_dt, 'b_dt': b_dt, 'A_log': A_log, 'D': D}
    _L0_attn_all = _L0_attn_setup()
    _L0_attn_in = {k: v for k, v in _L0_attn_all.items() if k in ('W_dbc', 'b_dbc', 'W_dt', 'b_dt', 'A_log', 'D')}
    del _L0_attn_all

    def _L0_xattn_setup():
        import jax, jax.numpy as jnp
        import numpy as np
        key = jax.random.key(seed)
        k1, k2, k3 = jax.random.split(key, 3)
        B, S, D, M = (8, 512, 512, 128)
        hidden_states = jax.random.normal(k1, (B, S, D), dtype=jnp.float32)
        memory_tokens = jax.random.normal(k2, (B, M, D), dtype=jnp.float32)
        memory_mask = jax.random.randint(k3, (B, M), 0, 2).astype(jnp.bool_)
        return {'hidden_states': hidden_states, 'memory_tokens': memory_tokens, 'memory_mask': memory_mask}
    _L0_xattn_all = _L0_xattn_setup()
    _L0_xattn_in = {k: v for k, v in _L0_xattn_all.items() if k in ()}
    del _L0_xattn_all

    def _L0_ffn_setup():
        import math
        import jax, jax.numpy as jnp
        import numpy as np
        DIM = 512
        RANK = 8
        B, T = (4, 1024)

        def _orthogonal(key, n):
            a = jax.random.normal(key, (n, n), dtype=jnp.float32)
            q, r = jnp.linalg.qr(a)
            q = q * jnp.sign(jnp.diagonal(r))[None, :]
            return q
        key = jax.random.key(seed)
        kx, kf = jax.random.split(key)
        x = jax.random.normal(kx, (B, T, DIM), dtype=jnp.float32)
        fkeys = jax.random.split(kf, RANK)
        factors = jnp.stack([_orthogonal(fkeys[r], DIM) * (r + 1) ** (-0.5) for r in range(RANK)])
        bias = jnp.zeros((DIM,), dtype=jnp.float32)
        return {'x': x, 'factors': factors, 'bias': bias}
    _L0_ffn_all = _L0_ffn_setup()
    _L0_ffn_in = {k: v for k, v in _L0_ffn_all.items() if k in ('factors', 'bias')}
    del _L0_ffn_all
    return {'x': x, 'ctx_2048': ctx_2048, 'mask_BxS2_bk0': mask_BxS2_bk0, 'L0_attn_W_dbc': _L0_attn_in['W_dbc'], 'L0_attn_b_dbc': _L0_attn_in['b_dbc'], 'L0_attn_W_dt': _L0_attn_in['W_dt'], 'L0_attn_b_dt': _L0_attn_in['b_dt'], 'L0_attn_A_log': _L0_attn_in['A_log'], 'L0_attn_D': _L0_attn_in['D'], 'L0_ffn_factors': _L0_ffn_in['factors'], 'L0_ffn_bias': _L0_ffn_in['bias']}

def reference(x, ctx_2048, mask_BxS2_bk0, L0_attn_W_dbc, L0_attn_b_dbc, L0_attn_W_dt, L0_attn_b_dt, L0_attn_A_log, L0_attn_D, L0_ffn_factors, L0_ffn_bias):
    import jax
    import jax.numpy as jnp

    def _L0_attn_ref(x, W_dbc, b_dbc, W_dt, b_dt, A_log, D):
        import jax, jax.numpy as jnp
        import numpy as np
        DT_RANK = 128
        DIM_INNER = 512
        D_STATE = 16
        IN_FEATURES = 512

        def _scan_combine(e1, e2):
            a1, b1 = e1
            a2, b2 = e2
            return (a1 * a2, a2 * b1 + b2)
        A = -jnp.exp(A_log)
        deltaBC = x @ W_dbc.T + b_dbc
        delta_lo = deltaBC[..., :DT_RANK]
        Bmat = deltaBC[..., DT_RANK:DT_RANK + D_STATE]
        Cmat = deltaBC[..., DT_RANK + D_STATE:]
        delta = jax.nn.softplus(delta_lo @ W_dt.T + b_dt)
        deltaA = jnp.exp(delta[..., None] * A)
        BX = delta[..., None] * Bmat[:, :, None, :] * x[..., None]
        _, hs = jax.lax.associative_scan(_scan_combine, (deltaA, BX), axis=1)
        y = jnp.einsum('blds,bls->bld', hs, Cmat) + D * x
        return y

    def _L0_xattn_ref(hidden_states, memory_tokens, memory_mask):
        import jax, jax.numpy as jnp
        import numpy as np
        B, S, D = hidden_states.shape
        scale = 1.0 / jnp.sqrt(jnp.asarray(D, hidden_states.dtype))
        scores = jnp.einsum('bsd,bmd->bsm', hidden_states, memory_tokens) * scale
        neg_inf = jnp.asarray(-1e+30, scores.dtype)
        scores = jnp.where(memory_mask[:, None, :], scores, neg_inf)
        attn = jax.nn.softmax(scores, axis=-1)
        readout = jnp.einsum('bsm,bmd->bsd', attn, memory_tokens)
        valid_b = jnp.any(memory_mask, axis=-1)
        out = jnp.where(valid_b[:, None, None], readout, jnp.zeros_like(readout))
        return out

    def _L0_ffn_ref(x, factors, bias):
        import math
        import jax, jax.numpy as jnp
        import numpy as np
        DIM = 512
        RANK = 8
        B, T = (4, 1024)

        def _orthogonal(key, n):
            a = jax.random.normal(key, (n, n), dtype=jnp.float32)
            q, r = jnp.linalg.qr(a)
            q = q * jnp.sign(jnp.diagonal(r))[None, :]
            return q
        rank = factors.shape[0]
        mixed = jnp.einsum('btd,rde->bte', x, factors)
        mixed = mixed / math.sqrt(rank) + bias
        return mixed
    x = _layernorm(x + _L0_attn_ref(x, L0_attn_W_dbc, L0_attn_b_dbc, L0_attn_W_dt, L0_attn_b_dt, L0_attn_A_log, L0_attn_D), axis=-1)
    x = _layernorm(x + _L0_xattn_ref(x, ctx_2048, mask_BxS2_bk0), axis=-1)
    x = _layernorm(x + _L0_ffn_ref(x, L0_ffn_factors, L0_ffn_bias), axis=-1)
    return x

_drawn_inputs = setup_inputs


def setup_inputs(seed=0):
    import zlib

    import numpy as np

    out = dict(_drawn_inputs(seed))
    spreads = {'L0_attn_D': (1.0, 0.2), 'L0_ffn_bias': (0.0, 0.1)}
    factors = {'L0_attn_b_dbc': 4.014, 'L0_attn_b_dt': 8.0}
    for name, (base, spread) in spreads.items():
        noise = np.random.default_rng([zlib.crc32(name.encode()), seed]).standard_normal(out[name].shape)
        drawn = base * np.exp(spread * noise) if base else spread * noise
        out[name] = jnp.asarray(drawn.astype(out[name].dtype))
    for name, factor in factors.items():
        out[name] = (out[name] * factor).astype(out[name].dtype)
    return out
```

```python
from contextlib import ExitStack

import concourse.bass as bass
from concourse import mybir

F32 = mybir.dt.float32
U8 = mybir.dt.uint8
ACT = mybir.ActivationFunctionType
ALU = mybir.AluOpType
AX_X = mybir.AxisListType.X

P = 128
NT = 16
D = 512
C = D // P
S = 16
R = 128
RANK = 8
G = 4
NG = NT // G
W = G * P
Q = 4
U = Q * C
IT = S // Q
GU = S * C
RA = 8
RH = 8
LAG = 4
EPS = 1e-5
BIG = 1e30
SCALE = float(D) ** -0.5
FSCALE = float(RANK) ** -0.5


def at_least(eng, sem, value):
    if isinstance(value, int) and value <= 0:
        return
    eng.wait_ge(sem, value)


def one(i):
    return bass.ds(i, 1)


def decoder_layer(nc, x, xT, ctx, ctxT, mask, WdbcT, b_lo, b_bc, WdtT, b_dt, A_log, Dv, factors, bias, ident, sel4,
                  cT, out):
    with ExitStack() as stack:
        def sb(name, *shape, dt=F32):
            return stack.enter_context(nc.sbuf_tensor(name, list(shape), dt))

        def ps(name, *shape):
            return stack.enter_context(nc.psum_tensor(name, list(shape), F32))

        def sem(name):
            return stack.enter_context(nc.semaphore(name))

        ident_sb = sb("ident_sb", P, P)
        sel_sb = sb("sel_sb", C, D)
        WdbcT_sb = sb("WdbcT_sb", P, C, R + 2 * S)
        WdtT_sb = sb("WdtT_sb", P, D)
        blo_sb = sb("blo_sb", P, 1)
        bbc_sb = sb("bbc_sb", 1, 2 * S)
        bdt_sb = sb("bdt_sb", C, P)
        A_sb = sb("A_sb", P, C, S)
        D1_sb = sb("D1_sb", P, C)
        bias_sb = sb("bias_sb", 1, D)
        ones_sb = sb("ones_sb", 1, P)
        mhalf_sb = sb("mhalf_sb", P, 1)
        mask_sb = sb("mask_sb", P, NT * P, dt=U8)
        neg_sb = sb("neg_sb", P, NT * P)
        best_sb = sb("best_sb", P, NT)
        valid_sb = sb("valid_sb", P, NT)
        F_sb = sb("F_sb", P, C, D)
        fac_sb = sb("fac_sb", P, RANK, D)
        x_in = sb("x_in", P, D)
        xT_in = sb("xT_in", P, C, P)
        xd_sb = sb("xd_sb", P, G, C, P)
        lo_sb = sb("lo_sb", P, P)
        bc_sb = sb("bc_sb", P, 2 * S)
        ct_sb = sb("ct_sb", S, P)
        sp_sb = sb("sp_sb", P, D)
        delta_t = sb("delta_t", P, C, P)
        delta_sb = sb("delta_sb", P, 2, C, G, P)
        dx_sb = sb("dx_sb", P, 2, G, D)
        B_sb = sb("B_sb", P, NG, S, G)
        C_sb = sb("C_sb", P, Q, W)
        prod_sb = sb("prod_sb", P, Q, G, D)
        a_sb = sb("a_sb", P, RA, G, P)
        h_sb = sb("h_sb", P, RH, W)
        z1_sb = sb("z1_sb", P, G, D)
        x1_sb = sb("x1_sb", P, D)
        x1T_sb = sb("x1T_sb", P, C, P)
        ctx_in = sb("ctx_in", P, D)
        ctxT_in = sb("ctxT_in", P, C, P)
        sc_sb = sb("sc_sb", P, P)
        p_sb = sb("p_sb", P, P)
        pn_sb = sb("pn_sb", P, P)
        pT_sb = sb("pT_sb", P, P)
        x2_sb = sb("x2_sb", P, D)
        x2T_sb = sb("x2T_sb", P, C, P)
        o_sb = sb("o_sb", P, D)
        st_sb = sb("st_sb", P, 3, 6)
        mv_sb = sb("mv_sb", P, 3, 2)
        ve_sb = sb("ve_sb", P, 3)
        rstd_sb = sb("rstd_sb", P, 3)
        nmr_sb = sb("nmr_sb", P, 1)
        mx_sb = sb("mx_sb", P, 1)
        nmx_sb = sb("nmx_sb", P, 1)
        sum_sb = sb("sum_sb", P, 1)
        rs_sb = sb("rs_sb", P, 1)
        rv_sb = sb("rv_sb", P, 1)

        bx_ps = ps("bx_ps", P, 2, W)
        y_ps = ps("y_ps", P, G, D)
        pj_ps = ps("pj_ps", P, D)
        at_ps = ps("at_ps", P, D)

        weights_in, consts_in, alog_in, x_loaded, xT_loaded = map(
            sem, ("weights_in", "consts_in", "alog_in", "x_loaded", "xT_loaded"))
        ctx_loaded, ctxT_loaded, fac_loaded = map(sem, ("ctx_loaded", "ctxT_loaded", "fac_loaded"))
        C_loaded = [sem(f"C{q}_loaded") for q in range(Q)]
        ct_stored, delta_stored, out_stored = map(sem, ("ct_stored", "delta_stored", "out_stored"))
        zeroed, A_exp, A_ready, D1_ready, neg_ready, best_ready, valid_ready, ones_ready, mhalf_ready = map(
            sem, ("zeroed", "A_exp", "A_ready", "D1_ready", "neg_ready", "best_ready", "valid_ready", "ones_ready",
                  "mhalf_ready"))
        fsum_ready, fsum_copied, F_ready = map(sem, ("fsum_ready", "fsum_copied", "F_ready"))
        lo_ready, bc_copied, b_stored, ct_ready, ct_copied, z_ready = map(
            sem, ("lo_ready", "bc_copied", "b_stored", "ct_ready", "ct_copied", "z_ready"))
        abs_done, spexp_done, spln_done, delta_ready, dT_ready, dx_ready, xd_ready = map(
            sem, ("abs_done", "spexp_done", "spln_done", "delta_ready", "dT_ready", "dx_ready", "xd_ready"))
        prod_ready, a_ready, bx_ready, h_ready, hc_ready, y_added = map(
            sem, ("prod_ready", "a_ready", "bx_ready", "h_ready", "hc_ready", "y_added"))
        skip_added, z1_by_dve, z1_by_act = map(sem, ("skip_added", "z1_by_dve", "z1_by_act"))
        st_done = [sem(f"st{n}_done") for n in range(3)]
        mv_done = [sem(f"mv{n}_done") for n in range(3)]
        ve_done = [sem(f"ve{n}_done") for n in range(3)]
        rstd_done = [sem(f"rstd{n}_done") for n in range(3)]
        x1_ready, x1T_ready, x1T_copied, scores_ready, masked, max_done, nmx_ready, p_ready = map(
            sem, ("x1_ready", "x1T_ready", "x1T_copied", "scores_ready", "masked", "max_done", "nmx_ready",
                  "p_ready"))
        rs_done, rv_done, pn_ready, pT_ready, pT_copied, z2_ready, nmr_ready, x2_ready = map(
            sem, ("rs_done", "rv_done", "pn_ready", "pT_ready", "pT_copied", "z2_ready", "nmr_ready", "x2_ready"))
        x2T_ready, x2T_copied, z3_ready, o_ready = map(sem, ("x2T_ready", "x2T_copied", "z3_ready", "o_ready"))

        waits_carried = sem("waits_carried")

        N_WEIGHTS, N_CONSTS = 2, 9

        def at_least_alone(eng, sem, value):
            at_least(eng, sem, value)
            if not isinstance(value, int):
                eng.sem_inc(waits_carried, 1)

        block = stack.enter_context(nc.Block())

        def run_iterations(eng, iteration):
            for g in range(NG):
                peeled = {0: (0,), 1: (0, 1)}.get(g, (0,))
                for j in peeled:
                    iteration(g, j)
                last = IT - 1 if g == NG - 1 else IT
                with eng.Fori(len(peeled), last) as j:
                    iteration(g, j)
                if g == NG - 1:
                    iteration(g, IT - 1)

        def has_projection(g):
            return g < NG - 1

        def attention_tile(g, j):
            i = IT * g + j
            if g == 0 or (g == 1 and isinstance(j, int) and j == 0):
                return None
            if isinstance(j, int) and j == 0:
                return i - 5, G - 1
            return i - 5, j - 1

        def finishes_tile(g, j):
            return attention_tile(g, j) is not None and not (g == 1 and isinstance(j, int) and j == 1)

        @block.sync
        def _(sp):
            sp.dma_start(WdbcT_sb[:, :, :], WdbcT.rearrange("(c p) n -> p c n", p=P)).then_inc(weights_in, 16)
            sp.dma_start(WdtT_sb[:, :], WdtT).then_inc(weights_in, 16)

            def load_tile(t):
                at_least_alone(sp, lo_ready, t)
                at_least_alone(sp, xd_ready, t)
                sp.dma_start(xT_in[:, :, :], xT[one(t), :, :, :].rearrange("a p c n -> p (a c) n")
                             ).then_inc(xT_loaded, 16)
                at_least_alone(sp, dx_ready, t)
                sp.dma_start(x_in[:, :], x[one(t), :, :].rearrange("a p d -> p (a d)")).then_inc(x_loaded, 16)

            def store_projection(g, tile, t):
                at_least_alone(sp, ct_copied, t + 1)
                sp.dma_start(cT[g, :, one(tile), :].rearrange("s a n -> s (a n)"), ct_sb[:, :]
                             ).then_inc(ct_stored, 16)

            def store_delta(g, tile, t):
                at_least_alone(sp, delta_ready, t + 1)
                at_least_alone(sp, a_ready, GU * (g - 1))
                sp.dma_start(delta_sb[:, g % 2, :, one(tile), :].rearrange("p c a n -> p c (a n)"),
                             delta_t[:, :, :]).then_inc(delta_stored, 16)

            def load_C(i, q, stored):
                at_least_alone(sp, ct_stored, 16 * stored)
                at_least_alone(sp, hc_ready, U * (i - 1) + C * (q + 1))
                flat = cT.rearrange("g s b n -> (g s) (b n)")
                sp.dma_start(C_sb[:, q, :], flat[one(Q * i + q), :].to_broadcast((P, W))).then_inc(C_loaded[q], 16)

            load_tile(0)
            for dst, src in ((blo_sb[:, :], b_lo), (bbc_sb[:, :], b_bc), (bdt_sb[:, :], b_dt), (sel_sb[:, :], sel4),
                             (D1_sb[:, :], Dv), (bias_sb[:, :], bias),
                             (ident_sb[:, :], ident),
                             (A_sb[:, :, :], A_log.rearrange("(c p) s -> p c s", p=P)),
                             (mask_sb[:, :], mask.to_broadcast((P, NT * P)))):
                sp.dma_start(dst, src).then_inc(consts_in, 16)
            store_projection(0, 0, 0)
            store_delta(0, 0, 0)
            with sp.Fori(1, G) as t:
                load_tile(t)
                store_projection(0, t, t)
                store_delta(0, t, t)
            for q in range(Q):
                load_C(0, q, G)

            def iteration(g, j):
                i = IT * g + j
                if has_projection(g):
                    load_tile(i + G)
                if g == 0:
                    at_least_alone(sp, fsum_ready, j)
                    rows = factors[:, bass.ds(j * P, P), :] if not isinstance(j, int) else factors[:, j * P:(j + 1) * P, :]
                    sp.dma_start(fac_sb[:, :, :], rows.rearrange("r p e -> p r e")).then_inc(fac_loaded, 16)
                tile = attention_tile(g, j)
                if tile:
                    at_least_alone(sp, scores_ready, tile[0])
                    sp.dma_start(ctxT_in[:, :, :], ctxT[one(tile[0]), :, :, :].rearrange("a p c n -> p (a c) n")
                                 ).then_inc(ctxT_loaded, 16)
                    at_least_alone(sp, z2_ready, tile[0])
                    sp.dma_start(ctx_in[:, :], ctx[one(tile[0]), :, :].rearrange("a p d -> p (a d)")
                                 ).then_inc(ctx_loaded, 16)
                if tile and finishes_tile(g, j):
                    store_out(tile[0] - 1)
                if has_projection(g):
                    store_projection(g + 1, j, i + G)
                more = not (g == NG - 1 and isinstance(j, int) and j == IT - 1)
                if more:
                    load_C(i + 1, 0, i + G + 1 if has_projection(g) else NT)
                if has_projection(g):
                    store_delta(g + 1, j, i + G)
                for q in range(1, Q):
                    if more:
                        load_C(i + 1, q, 0)

            def store_out(t):
                at_least_alone(sp, o_ready, t + 1)
                sp.dma_start(out[one(t), :, :].rearrange("a p d -> p (a d)"), o_sb[:, :]).then_inc(out_stored, 16)

            run_iterations(sp, iteration)

            def tail_tile(t, first=False):
                at_least_alone(sp, scores_ready, t)
                sp.dma_start(ctxT_in[:, :, :], ctxT[one(t), :, :, :].rearrange("a p c n -> p (a c) n")
                             ).then_inc(ctxT_loaded, 16)
                at_least_alone(sp, z2_ready, t)
                sp.dma_start(ctx_in[:, :], ctx[one(t), :, :].rearrange("a p d -> p (a d)")
                             ).then_inc(ctx_loaded, 16)
                store_out(t - 1)

            tail_tile(NT - G - 1)
            with sp.Fori(NT - G, NT) as t:
                tail_tile(t)
            store_out(NT - 1)
            sp.wait_ge(out_stored, 16 * NT)

        @block.gpsimd
        def _(pool):
            nc.gpsimd.memset(ones_sb[:, :], 1.0).then_inc(ones_ready, 1)
            nc.gpsimd.memset(mhalf_sb[:, :], -0.5).then_inc(mhalf_ready, 1)
            pool.wait_ge(mhalf_ready, 1)
            pool.wait_ge(D1_ready, 1)

            def store_B(g, tile, t):
                at_least(pool, bc_copied, t + 1)
                nc.gpsimd.tensor_copy(B_sb[:, g, :, one(tile)].rearrange("p s a -> p (s a)"), bc_sb[:, 0:S]
                                      ).then_inc(b_stored, 1)

            def scale_x(g, tile, t):
                at_least(pool, xT_loaded, 16 * (t + 1))
                at_least(pool, skip_added, g)
                nc.gpsimd.tensor_tensor(xd_sb[:, one(tile), :, :].rearrange("p a c n -> p (a c) n"), xT_in[:, :, :],
                                        D1_sb[:, :].rearrange("p (c a) -> p c a", a=1).to_broadcast((P, C, P)),
                                        ALU.mult).then_inc(xd_ready, 1)

            def rstd(n, t):
                at_least(pool, ve_done[n], t + 1)
                nc.gpsimd.tensor_tensor(rstd_sb[:, n:n + 1], ve_sb[:, n:n + 1], mhalf_sb[:, :], ALU.pow
                                        ).then_inc(rstd_done[n], 1)

            scale_x(0, 0, 0)
            store_B(0, 0, 0)
            with pool.Fori(1, G) as t:
                scale_x(0, t, t)
                store_B(0, t, t)

            def iteration(g, j):
                i = IT * g + j
                tile = attention_tile(g, j)
                for u in range(U):
                    k = U * i + u
                    if tile and u == 1:
                        rstd(0, tile[0])
                    if tile and u == 9:
                        rstd(1, tile[0])
                    if tile and finishes_tile(g, j) and u == 0:
                        rstd(2, tile[0] - 1)
                    if u % C == 0:
                        at_least(pool, C_loaded[u // C], 16 * (i + 1))
                    at_least(pool, h_ready, k + 1)
                    h = h_sb[:, u % RH, :]
                    nc.gpsimd.tensor_tensor(h, h, C_sb[:, u // C, :], ALU.mult).then_inc(hc_ready, 1)
                    if has_projection(g) and u == 2:
                        store_B(g + 1, j, i + G)
                    if has_projection(g) and u == 6:
                        scale_x(g + 1, j, i + G)
                if g == 0:
                    at_least(pool, fsum_copied, j + 1)
                    diag = F_sb[:, :, :].rearrange("p c d -> p (c d)")
                    diag = diag[:, bass.ds(j * (D + P), P)] if not isinstance(j, int) else diag[:, j * (D + P):j * (D + P) + P]
                    nc.gpsimd.tensor_tensor(diag, diag, ident_sb[:, :], ALU.add).then_inc(F_ready, 1)

            run_iterations(pool, iteration)
            rstd(2, NT - G - 2)

            def tail_tile(t):
                rstd(0, t)
                rstd(1, t)
                rstd(2, t)

            tail_tile(NT - G - 1)
            with pool.Fori(NT - G, NT) as t:
                tail_tile(t)

        @block.scalar
        def _(act):
            nc.scalar.preload_act_table_set("natural_log_exp_and_others")
            act.wait_ge(consts_in, 16 * N_CONSTS)
            nc.scalar.activation(A_sb[:, :, :], A_sb[:, :, :], ACT.Exp).then_inc(A_exp, 1)

            def copy_lo(t):
                at_least(act, lo_ready, t + 1)
                nc.scalar.activation(lo_sb[:, :], pj_ps[:, 0:R], ACT.Identity, bias=blo_sb[:, :])
                at_least(act, b_stored, t)
                nc.scalar.activation(bc_sb[:, :], pj_ps[:, R:R + 2 * S], ACT.Copy).then_inc(bc_copied, 1)

            def sp_abs(t):
                at_least(act, z_ready, t + 1)
                nc.scalar.activation(sp_sb[:, :], pj_ps[:, :], ACT.Abs).then_inc(abs_done, 1)

            def sp_exp(t):
                at_least(act, abs_done, t + 1)
                nc.scalar.activation(sp_sb[:, :], sp_sb[:, :], ACT.Exp, scale=-1.0).then_inc(spexp_done, 1)

            def sp_ln(t):
                at_least(act, spexp_done, t + 1)
                nc.scalar.activation(sp_sb[:, :], sp_sb[:, :], ACT.Ln, bias=1.0).then_inc(spln_done, 1)

            def project(t):
                copy_lo(t)
                sp_abs(t)
                sp_exp(t)
                sp_ln(t)

            project(0)
            with act.Fori(1, G) as t:
                project(t)

            def product(half, n, q, b, slot_count):
                if b == 0:
                    at_least(act, bx_ready, slot_count)
                scale = B_sb[:, :, :, :].rearrange("p g s b -> p (g s b)")
                scale = scale[:, n * G + b:n * G + b + 1] if isinstance(n, int) else scale[:, bass.ds(n * G + b, 1)]
                src = dx_sb[:, half, b, :] if isinstance(half, int) else dx_sb[:, one(half), b, :].rearrange("p a d -> p (a d)")
                nc.scalar.activation(prod_sb[:, q, b, :], src, ACT.Copy, scale=scale).then_inc(prod_ready, 1)

            def x1T_copy(t):
                at_least(act, x1T_ready, t + 1)
                nc.scalar.activation(x1T_sb[:, :, :].rearrange("p c n -> p (c n)"), at_ps[:, :], ACT.Copy
                                     ).then_inc(x1T_copied, 1)

            def probs(t):
                at_least(act, nmx_ready, t + 1)
                nc.scalar.activation(p_sb[:, :], sc_sb[:, :], ACT.Exp, bias=nmx_sb[:, :], accum_out=sum_sb[:, :]
                                     ).then_inc(p_ready, 1)

            def pT_copy(t):
                at_least(act, pT_ready, t + 1)
                nc.scalar.activation(pT_sb[:, :], at_ps[:, 0:P], ACT.Copy).then_inc(pT_copied, 1)

            def x2_norm(t):
                at_least(act, nmr_ready, t + 1)
                nc.scalar.activation(x2_sb[:, :], at_ps[:, :], ACT.Identity, bias=nmr_sb[:, :],
                                     scale=rstd_sb[:, 1:2]).then_inc(x2_ready, 1)

            def x2T_copy(t):
                at_least(act, x2T_ready, t + 1)
                nc.scalar.activation(x2T_sb[:, :, :].rearrange("p c n -> p (c n)"), at_ps[:, :], ACT.Copy
                                     ).then_inc(x2T_copied, 1)

            def z1_copy(g, b):
                at_least(act, y_added, GU * (g + 1))
                at_least(act, x1_ready, G * g)
                nc.scalar.activation(z1_sb[:, b, :], y_ps[:, b, :], ACT.Copy).then_inc(z1_by_act, 1)

            act.wait_ge(dx_ready, G)
            act.wait_ge(b_stored, G)
            for b in range(G):
                product(0, 0, 0, b, 0)
            act.wait_ge(A_ready, 1)
            act.wait_ge(zeroed, 1)

            def iteration(g, j):
                i = IT * g + j
                tile = attention_tile(g, j)
                last = g == NG - 1 and isinstance(j, int) and j == IT - 1
                if isinstance(j, int) and j == 0:
                    act.wait_ge(delta_stored, 16 * G * (g + 1))
                for u in range(U):
                    k = U * i + u
                    q, c = u // C, u % C
                    at_least(act, h_ready, k - RA + 1)
                    s = Q * j + q
                    A_col = A_sb[:, c, s:s + 1] if isinstance(s, int) else A_sb[:, c, one(s)]
                    nc.scalar.activation(a_sb[:, u % RA, :, 1:], delta_sb[:, g % 2, c, :, 1:], ACT.Exp, scale=A_col
                                         ).then_inc(a_ready, 1)
                    if q < Q - 1:
                        product(g % 2, Q * i + q + 1, q + 1, c, U * (i - 1) + C * (q + 2))
                    elif not last:
                        if c == 0 and has_projection(g):
                            at_least(act, dx_ready, i + G + 1)
                            at_least(act, b_stored, i + G + 1)
                        half = ((i + 1) // IT) % 2 if isinstance(j, int) else (
                            (g % 2) if not has_projection(g) else (j + 1 + IT * g) // IT % 2)
                        product(half, Q * (i + 1), 0, c, U * i + C)
                    if has_projection(g):
                        if u == 2:
                            copy_lo(i + G)
                        if u == 5:
                            sp_abs(i + G)
                        if u == 6:
                            sp_exp(i + G)
                        if u == 7:
                            sp_ln(i + G)
                    if g == 0 and u == 12:
                        at_least(act, fsum_ready, j + 1)
                        nc.scalar.activation(F_sb[:, one(j), :].rearrange("p a d -> p (a d)"), at_ps[:, :], ACT.Copy,
                                             scale=FSCALE).then_inc(fsum_copied, 1)
                    if tile:
                        if u == 3:
                            x1T_copy(tile[0])
                        if u == 5:
                            probs(tile[0])
                        if u == 8:
                            pT_copy(tile[0])
                        if u == 10:
                            x2_norm(tile[0])
                        if u == 11:
                            x2T_copy(tile[0])
                    if g > 0 and isinstance(j, int) and j == 0 and u == LAG:
                        z1_copy(g - 1, 2)
                        z1_copy(g - 1, 3)

            run_iterations(act, iteration)

            def tail_tile(t):
                x1T_copy(t)
                probs(t)
                pT_copy(t)
                x2_norm(t)
                x2T_copy(t)

            tail_tile(NT - G - 1)
            z1_copy(NG - 1, 2)
            z1_copy(NG - 1, 3)
            with act.Fori(NT - G, NT) as t:
                tail_tile(t)

        @block.tensor
        def _(pe):
            pe.wait_ge(weights_in, 16 * N_WEIGHTS)
            pe.wait_ge(consts_in, 16 * N_CONSTS)
            pe.wait_ge(ones_ready, 1)

            def transpose(dst, src, start=True):
                return nc.tensor.matmul(dst, src, ident_sb[:, :], start=start, stop=True, is_transpose=True,
                                        skip_group_check=True)

            def proj_lo(t):
                at_least(pe, xT_loaded, 16 * (t + 1))
                at_least(pe, dx_ready, t)
                for c in range(C):
                    nc.tensor.matmul(pj_ps[:, 0:R], WdbcT_sb[:, c, 0:R], xT_in[:, c, :], start=c == 0, stop=c == C - 1)
                nc.tensor.matmul(pj_ps[:, R:R + 2 * S], ones_sb[:, :], bbc_sb[:, :], start=True, stop=False)
                for c in range(C):
                    last = nc.tensor.matmul(pj_ps[:, R:R + 2 * S], xT_in[:, c, :], WdbcT_sb[:, c, R:R + 2 * S],
                                            start=False, stop=c == C - 1)
                last.then_inc(lo_ready, 1)

            def proj_ct(t):
                at_least(pe, bc_copied, t + 1)
                transpose(pj_ps[0:S, 0:P], bc_sb[:, S:2 * S]).then_inc(ct_ready, 1)

            def proj_z(t):
                at_least(pe, ct_copied, t + 1)
                nc.tensor.matmul(pj_ps[:, :], bdt_sb[:, :], sel_sb[:, :], start=True, stop=False,
                                 skip_group_check=True)
                for c in range(C):
                    last = nc.tensor.matmul(pj_ps[:, c * P:(c + 1) * P], WdtT_sb[:, c * P:(c + 1) * P], lo_sb[:, :],
                                            start=False, stop=c == C - 1, skip_group_check=True)
                last.then_inc(z_ready, 1)

            def proj_dT(t):
                at_least(pe, delta_ready, t + 1)
                for c in range(C):
                    last = transpose(pj_ps[:, c * P:(c + 1) * P], delta_t[:, c, :])
                last.then_inc(dT_ready, 1)

            def project(t):
                proj_lo(t)
                proj_ct(t)
                proj_z(t)
                proj_dT(t)

            project(0)
            with pe.Fori(1, G) as t:
                project(t)

            def x1_transpose(t):
                at_least(pe, x1_ready, t + 1)
                at_least(pe, o_ready, t)
                for c in range(C):
                    last = transpose(at_ps[:, c * P:(c + 1) * P], x1_sb[:, c * P:(c + 1) * P])
                last.then_inc(x1T_ready, 1)

            def scores(t):
                at_least(pe, x1T_copied, t + 1)
                at_least(pe, ctxT_loaded, 16 * (t + 1))
                for c in range(C):
                    last = nc.tensor.matmul(at_ps[:, 0:P], x1T_sb[:, c, :], ctxT_in[:, c, :], start=c == 0,
                                            stop=c == C - 1)
                last.then_inc(scores_ready, 1)

            def p_transpose(t):
                at_least(pe, pn_ready, t + 1)
                transpose(at_ps[:, 0:P], pn_sb[:, :]).then_inc(pT_ready, 1)

            def readout(t):
                at_least(pe, pT_copied, t + 1)
                at_least(pe, ctx_loaded, 16 * (t + 1))
                nc.tensor.matmul(at_ps[:, :], pT_sb[:, :], ctx_in[:, :], start=True, stop=False, skip_group_check=True)
                for c in range(C):
                    last = transpose(at_ps[:, c * P:(c + 1) * P], x1T_sb[:, c, :], start=False)
                last.then_inc(z2_ready, 1)

            def x2_transpose(t):
                at_least(pe, x2_ready, t + 1)
                for c in range(C):
                    last = transpose(at_ps[:, c * P:(c + 1) * P], x2_sb[:, c * P:(c + 1) * P])
                last.then_inc(x2T_ready, 1)

            def ffn(t, c):
                if c == 0:
                    at_least(pe, x2T_copied, t + 1)
                    nc.tensor.matmul(at_ps[:, :], ones_sb[:, :], bias_sb[:, :], start=True, stop=False)
                last = nc.tensor.matmul(at_ps[:, :], x2T_sb[:, c, :], F_sb[:, c, :], start=False, stop=c == C - 1)
                if c == C - 1:
                    last.then_inc(z3_ready, 1)

            def unit_bx(g, j, u):
                i = IT * g + j
                q, c = u // C, u % C
                if c == 0:
                    at_least(pe, prod_ready, G * (Q * i + q + 1))
                at_least(pe, h_ready, U * i + u - 1)
                for b in range(G):
                    last = transpose(bx_ps[:, u % 2, b * P:(b + 1) * P], prod_sb[:, q, b, c * P:(c + 1) * P])
                last.then_inc(bx_ready, 1)

            def unit_y(k, u):
                at_least(pe, hc_ready, k + 1)
                c = u % C
                for b in range(G):
                    last = transpose(y_ps[:, b, c * P:(c + 1) * P], h_sb[:, u % RH, b * P:(b + 1) * P], start=False)
                last.then_inc(y_added, 1)

            def skip(g):
                at_least(pe, z1_by_dve, 2 * g)
                at_least(pe, z1_by_act, 2 * g)
                at_least(pe, xd_ready, G * (g + 1))
                for b in range(G):
                    for c in range(C):
                        last = transpose(y_ps[:, b, c * P:(c + 1) * P], xd_sb[:, b, c, :], start=c == 0)
                last.then_inc(skip_added, 1)

            def iteration(g, j):
                i = IT * g + j
                tile = attention_tile(g, j)
                for u in range(U):
                    unit_bx(g, j, u)
                    k = U * i + u - LAG
                    if isinstance(j, int) and j == 0 and u == LAG:
                        skip(g)
                    if not (isinstance(k, int) and k < 0):
                        unit_y(k, (u - LAG) % U)
                    if has_projection(g):
                        if u == 1:
                            proj_lo(i + G)
                        if u == 3:
                            proj_ct(i + G)
                        if u == 5:
                            proj_z(i + G)
                        if u == 9:
                            proj_dT(i + G)
                    if g == 0 and 2 <= u < 2 + RANK:
                        r = u - 2
                        if r == 0:
                            at_least(pe, fac_loaded, 16 * (j + 1))
                            at_least(pe, fsum_copied, j)
                        last = nc.tensor.matmul(at_ps[:, :], ident_sb[:, :], fac_sb[:, r, :], start=r == 0,
                                                stop=r == RANK - 1)
                        if r == RANK - 1:
                            last.then_inc(fsum_ready, 1)
                    if tile:
                        t = tile[0]
                        if u == 0 and isinstance(j, int) and (g, j) == (1, 1):
                            pe.wait_ge(F_ready, C)
                        if u == 3:
                            x1_transpose(t)
                        if u == 4:
                            scores(t)
                        if u == 7:
                            p_transpose(t)
                        if u == 8:
                            readout(t)
                        if u == 11:
                            x2_transpose(t)
                        if u >= 12:
                            ffn(t, u - 12)

            run_iterations(pe, iteration)
            for u in range(U - LAG, U):
                unit_y(GU * NG - U + u, u)

            def tail_tile(t):
                x1_transpose(t)
                scores(t)
                p_transpose(t)
                readout(t)
                x2_transpose(t)
                for c in range(C):
                    ffn(t, c)

            tail_tile(NT - G - 1)
            with pe.Fori(NT - G, NT) as t:
                tail_tile(t)

        @block.vector
        def _(dve):
            nc.vector.memset(a_sb[:, :, :, :], 0.0).then_inc(zeroed, 1)
            dve.wait_ge(consts_in, 16 * N_CONSTS)
            nc.vector.tensor_scalar(D1_sb[:, :], D1_sb[:, :], 1.0, None, ALU.add).then_inc(D1_ready, 1)
            dve.wait_ge(A_exp, 1)
            nc.vector.tensor_scalar(A_sb[:, :, :], A_sb[:, :, :], -1.0, None, ALU.mult).then_inc(A_ready, 1)
            nc.vector.tensor_scalar(neg_sb[:, :], mask_sb[:, :], BIG, BIG, ALU.mult, ALU.subtract
                                    ).then_inc(neg_ready, 1)
            dve.wait_ge(neg_ready, 1)
            nc.vector.reduce_max(best_sb[:, :], neg_sb[:, :].rearrange("p (b n) -> p b n", n=P), AX_X
                                 ).then_inc(best_ready, 1)
            dve.wait_ge(best_ready, 1)
            nc.vector.tensor_scalar(valid_sb[:, :], best_sb[:, :], 0.0, None, ALU.is_ge).then_inc(valid_ready, 1)
            dve.wait_ge(valid_ready, 1)

            def copy_ct(t):
                at_least(dve, ct_ready, t + 1)
                at_least(dve, ct_stored, 16 * t)
                nc.vector.tensor_copy(ct_sb[:, :], pj_ps[0:S, 0:P]).then_inc(ct_copied, 1)

            def softplus_end(t):
                at_least(dve, spln_done, t + 1)
                at_least(dve, delta_stored, 16 * t)
                nc.vector.scalar_tensor_tensor(delta_t[:, :, :].rearrange("p c n -> p (c n)"), pj_ps[:, :], 0.0,
                                               sp_sb[:, :], ALU.max, ALU.add).then_inc(delta_ready, 1)

            def delta_x(g, tile, t):
                at_least(dve, dT_ready, t + 1)
                at_least(dve, x_loaded, 16 * (t + 1))
                at_least(dve, prod_ready, G * S * (g - 1))
                nc.vector.tensor_tensor(dx_sb[:, g % 2, one(tile), :].rearrange("p a d -> p (a d)"), pj_ps[:, :],
                                        x_in[:, :], ALU.mult).then_inc(dx_ready, 1)

            def project(t):
                copy_ct(t)
                softplus_end(t)
                delta_x(0, t, t)

            project(0)
            with dve.Fori(1, G) as t:
                project(t)

            def stats(n, src, t):
                nc.vector.bn_stats(st_sb[:, n, :], src).then_inc(st_done[n], 1)
                at_least_alone(dve, st_done[n], t + 1)
                nc.vector.bn_aggr(mv_sb[:, n, :], st_sb[:, n, :]).then_inc(mv_done[n], 1)
                at_least(dve, mv_done[n], t + 1)
                nc.vector.tensor_scalar(ve_sb[:, n:n + 1], mv_sb[:, n, 1:2], EPS, None, ALU.add
                                        ).then_inc(ve_done[n], 1)

            def z1_stats(t, place):
                if isinstance(place, int):
                    at_least(dve, z1_by_act, 2 * (t // G + 1) if isinstance(t, int) else 2)
                stats(0, z1_sb[:, one(place), :].rearrange("p a d -> p (a d)"), t)

            def x1_norm(t, place):
                at_least(dve, rstd_done[0], t + 1)
                nc.vector.tensor_scalar(x1_sb[:, :], z1_sb[:, one(place), :].rearrange("p a d -> p (a d)"),
                                        mv_sb[:, 0, 0:1], rstd_sb[:, 0:1], ALU.subtract, ALU.mult
                                        ).then_inc(x1_ready, 1)

            def mask_and_max(t):
                at_least(dve, scores_ready, t + 1)
                neg = neg_sb[:, t * P:(t + 1) * P] if isinstance(t, int) else neg_sb[:, bass.ds(t * P, P)]
                nc.vector.scalar_tensor_tensor(sc_sb[:, :], at_ps[:, 0:P], SCALE, neg, ALU.mult, ALU.add
                                               ).then_inc(masked, 1)
                at_least(dve, masked, t + 1)
                nc.vector.reduce_max(mx_sb[:, :], sc_sb[:, :], AX_X).then_inc(max_done, 1)
                at_least(dve, max_done, t + 1)
                nc.vector.tensor_scalar(nmx_sb[:, :], mx_sb[:, :], -1.0, None, ALU.mult).then_inc(nmx_ready, 1)

            def normalise_probs(t):
                at_least(dve, p_ready, t + 1)
                nc.vector.reciprocal(rs_sb[:, :], sum_sb[:, :]).then_inc(rs_done, 1)
                at_least(dve, rs_done, t + 1)
                nc.vector.tensor_tensor(rv_sb[:, :], rs_sb[:, :], valid_sb[:, one(t)], ALU.mult).then_inc(rv_done, 1)
                at_least(dve, rv_done, t + 1)
                nc.vector.tensor_scalar(pn_sb[:, :], p_sb[:, :], rv_sb[:, :], None, ALU.mult).then_inc(pn_ready, 1)

            def z2_stats(t):
                at_least(dve, z2_ready, t + 1)
                stats(1, at_ps[:, :], t)

            def z2_shift(t):
                at_least(dve, rstd_done[1], t + 1)
                nc.vector.scalar_tensor_tensor(nmr_sb[:, :], mv_sb[:, 1, 0:1], -1.0, rstd_sb[:, 1:2], ALU.mult,
                                               ALU.mult).then_inc(nmr_ready, 1)

            def z3_stats(t):
                at_least(dve, z3_ready, t + 1)
                stats(2, at_ps[:, :], t)

            def z3_norm(t):
                at_least(dve, rstd_done[2], t + 1)
                at_least(dve, out_stored, 16 * t)
                nc.vector.tensor_scalar(o_sb[:, :], at_ps[:, :], mv_sb[:, 2, 0:1], rstd_sb[:, 2:3], ALU.subtract,
                                        ALU.mult).then_inc(o_ready, 1)

            def z1_copy(g, b):
                at_least(dve, y_added, GU * (g + 1))
                at_least(dve, x1_ready, G * g)
                nc.vector.tensor_copy(z1_sb[:, b, :], y_ps[:, b, :]).then_inc(z1_by_dve, 1)

            def iteration(g, j):
                i = IT * g + j
                tile = attention_tile(g, j)
                for u in range(U):
                    k = U * i + u
                    at_least(dve, a_ready, k + 1)
                    at_least(dve, bx_ready, k + 1)
                    at_least(dve, y_added, k - RH + 1)
                    nc.vector.tensor_tensor_scan(h_sb[:, u % RH, :], a_sb[:, u % RA, :, :].rearrange("p b n -> p (b n)"),
                                                 bx_ps[:, u % 2, :], 0.0, ALU.mult, ALU.add).then_inc(h_ready, 1)
                    if has_projection(g):
                        if u == 3:
                            copy_ct(i + G)
                        if u == 7:
                            softplus_end(i + G)
                        if u == 9:
                            delta_x(g + 1, j, i + G)
                    if tile:
                        t, place = tile
                        if u == 0:
                            if finishes_tile(g, j):
                                z3_norm(t - 1)
                            z1_stats(t, place)
                        if u == 1:
                            x1_norm(t, place)
                        if u == 4:
                            mask_and_max(t)
                        if u == 5:
                            normalise_probs(t)
                        if u == 8:
                            z2_stats(t)
                        if u == 9:
                            z2_shift(t)
                        if u == 15:
                            z3_stats(t)
                    if g > 0 and isinstance(j, int) and j == 0 and u == LAG - 1:
                        z1_copy(g - 1, 0)
                        z1_copy(g - 1, 1)

            run_iterations(dve, iteration)

            def tail_tile(t, place):
                z1_stats(t, place)
                x1_norm(t, place)
                mask_and_max(t)
                normalise_probs(t)
                z2_stats(t)
                z2_shift(t)
                z3_stats(t)
                z3_norm(t)

            z3_norm(NT - G - 2)
            tail_tile(NT - G - 1, G - 1)
            z1_copy(NG - 1, 0)
            z1_copy(NG - 1, 1)
            dve.wait_ge(z1_by_act, 2 * NG)
            dve.wait_ge(z1_by_dve, 2 * NG)
            with dve.Fori(NT - G, NT) as t:
                tail_tile(t, t - (NT - G))


def kernel(x, ctx_2048, mask_BxS2_bk0, L0_attn_W_dbc, L0_attn_b_dbc, L0_attn_W_dt, L0_attn_b_dt, L0_attn_A_log,
           L0_attn_D, L0_ffn_factors, L0_ffn_bias):
    import numpy as np
    import concourse.bacc as bacc
    from concourse import mybir as mb
    from concourse.bass_utils import run_bass_kernel_spmd

    def channels_first(v):
        v = np.asarray(v).transpose(0, 2, 1).reshape(NT, C, P, P)
        return np.ascontiguousarray(v.transpose(0, 2, 1, 3))

    b_dbc = np.asarray(L0_attn_b_dbc)
    arrays = {
        "x": np.asarray(x),
        "xT": channels_first(x),
        "ctx": np.asarray(ctx_2048),
        "ctxT": channels_first(ctx_2048),
        "mask": np.asarray(mask_BxS2_bk0).reshape(1, NT * P),
        "WdbcT": np.ascontiguousarray(np.asarray(L0_attn_W_dbc).T),
        "b_lo": np.ascontiguousarray(b_dbc[:R].reshape(P, 1)),
        "b_bc": np.ascontiguousarray(b_dbc[R:].reshape(1, 2 * S)),
        "WdtT": np.ascontiguousarray(np.asarray(L0_attn_W_dt).T),
        "b_dt": np.asarray(L0_attn_b_dt).reshape(C, P),
        "A_log": np.asarray(L0_attn_A_log),
        "Dv": np.ascontiguousarray(np.asarray(L0_attn_D).reshape(C, P).T),
        "factors": np.asarray(L0_ffn_factors),
        "bias": np.asarray(L0_ffn_bias).reshape(1, D),
        "ident": np.eye(P, dtype=np.float32),
        "sel4": np.repeat(np.eye(C, dtype=np.float32), P, axis=1),
    }
    nc = bacc.Bacc("TRN2", target_bir_lowering=False, num_devices=1)
    args = {n: nc.dram_tensor(f"in_{n}", v.shape, mb.dt.from_np(v.dtype), kind="ExternalInput").ap()
            for n, v in arrays.items()}
    cT = nc.dram_tensor("c_spread", (NG, S, G, P), F32, kind="Internal").ap()
    out = nc.dram_tensor("out", (NT, P, D), F32, kind="ExternalOutput").ap()
    decoder_layer(nc, cT=cT, out=out, **args)
    r = run_bass_kernel_spmd(nc, [{f"in_{n}": v for n, v in arrays.items()}], core_ids=[0])
    return r.results[0]["out"]
```

```python
from collections import namedtuple
from contextlib import ExitStack

import concourse.bass as bass
from concourse import mybir

F32 = mybir.dt.float32
BF16 = mybir.dt.bfloat16
U8 = mybir.dt.uint8
ACT = mybir.ActivationFunctionType
ALU = mybir.AluOpType
AX_X = mybir.AxisListType.X

P = 128
NT = 16
D = 512
C = D // P
S = 16
R = 128
RANK = 8
G = 4
NG = NT // G
W = G * P
Q = 4
U = Q * C
IT = S // Q
GU = S * C
RA = 8
RH = 8
LAG = 5
PARTS = 3
KB = 32 * PARTS
NB = D + 2 * S + P
PE_SLOT = dict(bc=1, lo=1, ct=2, z=(4, 5), dT=9, scores=0, pT=5, residual=6, readout=7, x2T=11,
               ffn=(13, 14, 14, 15), x1T=14)
DVE_SLOT = dict(copy_ct=3, softplus_end=8, delta_x=9, mask=0, normalise=3, z2_stats=7, z2_shift=8,
                z1_stats=10, x1_norm=13, z3_stats=15, z3_norm=0)
ACT_SLOT = dict(copy_lo=5, sp_abs=9, sp_exp=9, sp_ln=10, x1T=0, probs=6, pT=8, x2_norm=12, x2T=14, F=11, z1=7)
POOL_SLOT = dict(rstd0=11, rstd1=8, rstd2=0, store_B=3, scale_x=4)
FACTOR_SLOT = 2
EPS = 1e-5
BIG = 1e30
SCALE = float(D) ** -0.5
FSCALE = float(RANK) ** -0.5


Lane = namedtuple("Lane", "n bank ffn_bank x1 x1T ctx ctxT sc p pn pT x2 x2T o")


def at_least(eng, sem, value):
    if isinstance(value, int) and value <= 0:
        return
    eng.wait_ge(sem, value)


def one(i):
    return bass.ds(i, 1)


def decoder_layer(nc, x, xT, ctx, ctxT, mask, WdbcT, b_lo, b_bc, bias_rows, WdtT, A_log, Dv, factors, ident, sel_rows,
                  cT, out):
    with ExitStack() as stack:
        def sb(name, *shape, dt=F32):
            return stack.enter_context(nc.sbuf_tensor(name, list(shape), dt))

        def ps(name, *shape):
            return stack.enter_context(nc.psum_tensor(name, list(shape), F32))

        def sem(name):
            return stack.enter_context(nc.semaphore(name))

        ident_sb = sb("ident_sb", P, P)
        sel_raw = sb("sel_raw", KB, D)
        sel_sb = sb("sel_sb", KB, D, dt=BF16)
        WdbcT_sb = sb("WdbcT_sb", P, C, R + 2 * S)
        WdtT_sb = sb("WdtT_sb", P, D)
        blo_sb = sb("blo_sb", P, 1)
        bbc_sb = sb("bbc_sb", 2 * S, 1)
        A_sb = sb("A_sb", P, C, S)
        D1_sb = sb("D1_sb", P, C)
        raw_sb = sb("raw_sb", KB, NB)
        rest_sb = sb("rest_sb", KB, NB)
        part_sb = sb("part_sb", KB, NB, dt=BF16)
        biases_sb = sb("biases_sb", KB, NB, dt=BF16)
        ones_sb = sb("ones_sb", KB, P, dt=BF16)
        mhalf_sb = sb("mhalf_sb", P, 1)
        mask_sb = sb("mask_sb", P, NT * P, dt=U8)
        neg_sb = sb("neg_sb", P, NT * P)
        best_sb = sb("best_sb", P, NT)
        valid_sb = sb("valid_sb", P, NT)
        F_sb = sb("F_sb", P, C, D)
        fac_sb = sb("fac_sb", P, RANK, D)
        x_in = sb("x_in", P, D)
        xT_in = sb("xT_in", P, C, P)
        xd_sb = sb("xd_sb", P, G, C, P)
        lo_sb = sb("lo_sb", P, P)
        bc_sb = sb("bc_sb", P, 2 * S)
        ct_sb = sb("ct_sb", S, P)
        sp_sb = sb("sp_sb", P, D)
        delta_t = sb("delta_t", P, C, P)
        delta_sb = sb("delta_sb", P, 2, C, G, P)
        dx_sb = sb("dx_sb", P, 2, G, D)
        B_sb = sb("B_sb", P, NG, S, G)
        C_sb = sb("C_sb", P, Q, W)
        prod_sb = sb("prod_sb", P, Q, G, D)
        a_sb = sb("a_sb", P, RA, G, P)
        h_sb = sb("h_sb", P, RH, W)
        z1_sb = sb("z1_sb", P, G, D)
        x1_sb = sb("x1_sb", P, D)
        x1T_sb = sb("x1T_sb", P, C, P)
        ctx_in = sb("ctx_in", P, D)
        ctxT_in = sb("ctxT_in", P, C, P)
        sc_sb = sb("sc_sb", P, P)
        p_sb = sb("p_sb", P, P)
        pn_sb = sb("pn_sb", P, P)
        pT_sb = sb("pT_sb", P, P)
        x2_sb = sb("x2_sb", P, D)
        x2T_sb = sb("x2T_sb", P, C, P)
        o_sb = sb("o_sb", P, D)
        st_sb = sb("st_sb", P, G + 1, 3, 6)
        mv_sb = sb("mv_sb", P, G + 1, 3, 2)
        ve_sb = sb("ve_sb", P, G + 1, 3)
        rstd_sb = sb("rstd_sb", P, G + 1, 3)
        nmr_sb = sb("nmr_sb", P, G + 1)
        mx_sb = sb("mx_sb", P, G + 1)
        nmx_sb = sb("nmx_sb", P, G + 1)
        sum_sb = sb("sum_sb", P, G + 1)
        rs_sb = sb("rs_sb", P, G + 1)
        rv_sb = sb("rv_sb", P, G + 1)

        def first_xT(b):
            return prod_sb[:, 1, b, :].rearrange("p (c n) -> p c n", n=P)

        def first_x(b):
            return prod_sb[:, 2, b, :]

        def first_sp(b):
            return prod_sb[:, 3, b, :]

        first_lo = h_sb[:, 0, :]
        first_bcT = C_sb[0:2 * S, Q - 1, :]

        bx_ps = ps("bx_ps", P, 2, W)
        y_ps = ps("y_ps", P, G, D)
        pj_ps = ps("pj_ps", P, D)
        at_ps = ps("at_ps", P, D)

        def in_chunks(v):
            return v.rearrange("p (c n) -> p c n", n=P)

        lane = Lane(n=0, bank=at_ps[:, :], ffn_bank=pj_ps[:, :], x1=x1_sb[:, :], x1T=x1T_sb[:, :, :], ctx=ctx_in[:, :],
                    ctxT=ctxT_in[:, :, :], sc=sc_sb[:, :], p=p_sb[:, :], pn=pn_sb[:, :], pT=pT_sb[:, :], x2=x2_sb[:, :],
                    x2T=x2T_sb[:, :, :], o=o_sb[:, :])
        last_lanes = [Lane(n=b + 1, bank=y_ps[:, b, :], ffn_bank=y_ps[:, b, :], x1=prod_sb[:, 0, b, :],
                           x1T=in_chunks(prod_sb[:, 1, b, :]), ctx=fac_sb[:, b, :], ctxT=in_chunks(fac_sb[:, G + b, :]),
                           sc=a_sb[:, 0, b, :], p=a_sb[:, 1, b, :], pn=a_sb[:, 2, b, :], pT=a_sb[:, 3, b, :],
                           x2=prod_sb[:, 2, b, :], x2T=in_chunks(prod_sb[:, 3, b, :]), o=h_sb[:, b, :])
                      for b in range(G)]
        before_last = (NT - G - 1, lane)
        last_tiles = [(NT - G + b, last_lanes[b]) for b in range(G)]

        Wdbc_in, Wdt_in, blo_in, ident_in, Dv_in, alog_in, mask_in, x_loaded, xT_loaded = map(
            sem, ("Wdbc_in", "Wdt_in", "blo_in", "ident_in", "Dv_in", "alog_in", "mask_in", "x_loaded",
                  "xT_loaded"))
        first_xT_in = [sem(f"first_xT{c}_in") for c in range(C)]
        first_x_in, bbc_in, sel_in, BT_ready = map(sem, ("first_x_in", "bbc_in", "sel_in", "BT_ready"))
        ctx_loaded, ctxT_loaded, fac_loaded = map(sem, ("ctx_loaded", "ctxT_loaded", "fac_loaded"))
        last_ctx_in = sem("last_ctx_in")
        C_loaded = [sem(f"C{q}_loaded") for q in range(Q)]
        ct_stored, delta_stored, out_stored = map(sem, ("ct_stored", "delta_stored", "out_stored"))
        zeroed, A_exp, A_ready, D1_ready, neg_ready, best_ready, valid_ready, ones_ready, mhalf_ready, sel_ready = map(
            sem, ("zeroed", "A_exp", "A_ready", "D1_ready", "neg_ready", "best_ready", "valid_ready", "ones_ready",
                  "mhalf_ready", "sel_ready"))
        biases_in, bias_step, biases_ready = map(sem, ("biases_in", "bias_step", "biases_ready"))
        fac_added, fsum_copied, F_ready = map(sem, ("fac_added", "fsum_copied", "F_ready"))
        lo_ready, bc_copied, b_stored, ct_ready, ct_copied, z_ready = map(
            sem, ("lo_ready", "bc_copied", "b_stored", "ct_ready", "ct_copied", "z_ready"))
        abs_done, spexp_done, spln_done, delta_ready, dT_ready, dx_ready, xd_ready = map(
            sem, ("abs_done", "spexp_done", "spln_done", "delta_ready", "dT_ready", "dx_ready", "xd_ready"))
        prod_ready, a_ready, bx_ready, h_ready, hc_ready, y_added = map(
            sem, ("prod_ready", "a_ready", "bx_ready", "h_ready", "hc_ready", "y_added"))
        skip_added, z1_by_dve, z1_by_act = map(sem, ("skip_added", "z1_by_dve", "z1_by_act"))
        st_done = [sem(f"st{n}_done") for n in range(3)]
        mv_done = [sem(f"mv{n}_done") for n in range(3)]
        ve_done = [sem(f"ve{n}_done") for n in range(3)]
        rstd_done = [sem(f"rstd{n}_done") for n in range(3)]
        x1_ready, x1T_ready, x1T_copied, scores_ready, masked, max_done, nmx_ready, p_ready = map(
            sem, ("x1_ready", "x1T_ready", "x1T_copied", "scores_ready", "masked", "max_done", "nmx_ready",
                  "p_ready"))
        rs_done, rv_done, pn_ready, pT_ready, pT_copied, z2_ready, nmr_ready, x2_ready = map(
            sem, ("rs_done", "rv_done", "pn_ready", "pT_ready", "pT_copied", "z2_ready", "nmr_ready", "x2_ready"))
        x2T_ready, x2T_copied, z3_ready, o_ready = map(sem, ("x2T_ready", "x2T_copied", "z3_ready", "o_ready"))

        waits_carried = sem("waits_carried")

        def loads(t):
            return 16 * (t + 1 - G)

        def at_least_alone(eng, sem, value):
            at_least(eng, sem, value)
            if not isinstance(value, int):
                eng.sem_inc(waits_carried, 1)

        block = stack.enter_context(nc.Block())

        def run_iterations(eng, iteration):
            for g in range(NG):
                peeled = {0: (0,), 1: (0, 1)}.get(g, (0,))
                for j in peeled:
                    iteration(g, j)
                last = IT - 1 if g == NG - 1 else IT
                with eng.Fori(len(peeled), last) as j:
                    iteration(g, j)
                if g == NG - 1:
                    iteration(g, IT - 1)

        def has_projection(g):
            return g < NG - 1

        def attention_tile(g, j):
            if g == 0 or (g == 1 and isinstance(j, int) and j == 0):
                return None
            return IT * g + j - G - 1

        def prepares_x1(g):
            return g > 0

        def finishes_tile(g, j):
            return attention_tile(g, j) is not None and not (g == 1 and isinstance(j, int) and j == 1)

        @block.sync
        def _(sp):
            sp.dma_start(WdbcT_sb[:, :, :], WdbcT.rearrange("(c p) n -> p c n", p=P)).then_inc(Wdbc_in, 16)
            for c in range(C):
                sp.dma_start(prod_sb[:, 1, :, c * P:(c + 1) * P], xT[0:G, :, c, :].rearrange("b p n -> p b n")
                             ).then_inc(first_xT_in[c], 16)
            sp.dma_start(A_sb[:, :, :], A_log.rearrange("(c p) s -> p c s", p=P)).then_inc(alog_in, 16)
            sp.dma_start(prod_sb[:, 2, :, :], x[0:G, :, :].rearrange("b p d -> p b d")).then_inc(first_x_in, 16)
            sp.dma_start(mask_sb[:, :], mask.to_broadcast((P, NT * P))).then_inc(mask_in, 16)

            def load_tile(t):
                at_least_alone(sp, lo_ready, t)
                at_least_alone(sp, xd_ready, t)
                sp.dma_start(xT_in[:, :, :], xT[one(t), :, :, :].rearrange("a p c n -> p (a c) n")
                             ).then_inc(xT_loaded, 16)
                at_least_alone(sp, dx_ready, t)
                sp.dma_start(x_in[:, :], x[one(t), :, :].rearrange("a p d -> p (a d)")).then_inc(x_loaded, 16)

            def store_projection(g, tile, t):
                at_least_alone(sp, ct_copied, t + 1)
                sp.dma_start(cT[g, :, one(tile), :].rearrange("s a n -> s (a n)"), ct_sb[:, :]
                             ).then_inc(ct_stored, 16)

            def store_delta(g, tile, t):
                at_least_alone(sp, delta_ready, t + 1)
                at_least_alone(sp, a_ready, GU * (g - 1))
                sp.dma_start(delta_sb[:, g % 2, :, one(tile), :].rearrange("p c a n -> p c (a n)"),
                             delta_t[:, :, :]).then_inc(delta_stored, 16)

            def load_ctx(t):
                at_least_alone(sp, scores_ready, t)
                sp.dma_start(ctxT_in[:, :, :], ctxT[one(t), :, :, :].rearrange("a p c n -> p (a c) n")
                             ).then_inc(ctxT_loaded, 16)
                at_least_alone(sp, z2_ready, t)
                sp.dma_start(ctx_in[:, :], ctx[one(t), :, :].rearrange("a p d -> p (a d)")
                             ).then_inc(ctx_loaded, 16)

            def load_C(i, q, stored):
                at_least_alone(sp, ct_stored, loads(stored))
                at_least_alone(sp, hc_ready, U * (i - 1) + C * (q + 1))
                flat = cT.rearrange("g s b n -> (g s) (b n)")
                sp.dma_start(C_sb[:, q, :], flat[one(Q * i + q), :].to_broadcast((P, W))).then_inc(C_loaded[q], 16)

            sp.wait_ge(ct_copied, G)
            sp.dma_start(cT[0, :, :, :].rearrange("s b n -> s (b n)"), first_bcT[S:2 * S, :]).then_inc(ct_stored, 16)
            for q in range(Q - 1):
                load_C(0, q, G)

            def iteration(g, j):
                i = IT * g + j
                if has_projection(g):
                    load_tile(i + G)
                if g == 0:
                    at_least_alone(sp, fsum_copied, j)
                    rows = factors[:, bass.ds(j * P, P), :] if not isinstance(j, int) else factors[:, j * P:(j + 1) * P, :]
                    sp.dma_start(fac_sb[:, :, :], rows.rearrange("r p e -> p r e")).then_inc(fac_loaded, 16)
                tile = attention_tile(g, j)
                if g == NG - 1 and isinstance(j, int) and j == 0:
                    sp.wait_ge(fsum_copied, C)
                    sp.dma_start(fac_sb[:, 0:G, :], ctx[NT - G:NT, :, :].rearrange("b p d -> p b d")
                                 ).then_inc(last_ctx_in, 16)
                    sp.dma_start(fac_sb[:, G:2 * G, :].rearrange("p b (c n) -> p b c n", n=P),
                                 ctxT[NT - G:NT, :, :, :].rearrange("b p c n -> p b c n")).then_inc(last_ctx_in, 16)
                if tile is not None:
                    load_ctx(tile)
                load_C(i, Q - 1, 0)
                if tile is not None and finishes_tile(g, j):
                    store_out(tile - 1, lane)
                if has_projection(g):
                    store_projection(g + 1, j, i + G)
                if g == NG - 1 and isinstance(j, int) and j == IT - 1:
                    load_ctx(NT - G - 1)
                more = not (g == NG - 1 and isinstance(j, int) and j == IT - 1)
                if more:
                    load_C(i + 1, 0, i + G + 1 if has_projection(g) else NT)
                if has_projection(g):
                    store_delta(g + 1, j, i + G)
                for q in range(1, Q - 1):
                    if more:
                        load_C(i + 1, q, 0)

            def store_out(t, place):
                at_least_alone(sp, o_ready, t + 1)
                sp.dma_start(out[one(t), :, :].rearrange("a p d -> p (a d)"), place.o).then_inc(out_stored, 16)

            run_iterations(sp, iteration)

            store_out(NT - G - 2, lane)
            for t, place in (before_last, *last_tiles):
                store_out(t, place)
            sp.wait_ge(out_stored, 16 * NT)

        @block.gpsimd
        def _(pool):
            nc.gpsimd.memset(ones_sb[:, :], 1.0).then_inc(ones_ready, 1)
            nc.gpsimd.memset(mhalf_sb[:, :], -0.5).then_inc(mhalf_ready, 1)
            pool.wait_ge(mhalf_ready, 1)

            def store_B(g, tile, t):
                at_least(pool, bc_copied, t + 1)
                nc.gpsimd.tensor_copy(B_sb[:, g, :, one(tile)].rearrange("p s a -> p (s a)"), bc_sb[:, 0:S]
                                      ).then_inc(b_stored, 1)

            def scale_x(g, tile, t):
                at_least(pool, xT_loaded, loads(t))
                at_least(pool, skip_added, g)
                nc.gpsimd.tensor_tensor(xd_sb[:, one(tile), :, :].rearrange("p a c n -> p (a c) n"), xT_in[:, :, :],
                                        D1_sb[:, :].rearrange("p (c a) -> p c a", a=1).to_broadcast((P, C, P)),
                                        ALU.mult).then_inc(xd_ready, 1)

            def rstd(n, t, place=lane):
                at_least(pool, ve_done[n], t + 1)
                nc.gpsimd.tensor_tensor(rstd_sb[:, place.n, n:n + 1], ve_sb[:, place.n, n:n + 1], mhalf_sb[:, :],
                                        ALU.pow).then_inc(rstd_done[n], 1)

            pool.wait_ge(D1_ready, 1)
            for c in range(C):
                pool.wait_ge(first_xT_in[c], 16)
            for b in range(G):
                nc.gpsimd.tensor_tensor(xd_sb[:, b, :, :], first_xT(b),
                                        D1_sb[:, :].rearrange("p (c a) -> p c a", a=1).to_broadcast((P, C, P)),
                                        ALU.mult).then_inc(xd_ready, 1)
            def iteration(g, j):
                i = IT * g + j
                tile = attention_tile(g, j)
                for u in range(U):
                    k = U * i + u
                    if tile is not None and finishes_tile(g, j) and u == POOL_SLOT["rstd2"]:
                        rstd(2, tile - 1)
                    if tile is not None and u == POOL_SLOT["rstd1"]:
                        rstd(1, tile)
                    if prepares_x1(g) and u == POOL_SLOT["rstd0"]:
                        rstd(0, i - G)
                    if u % C == 0:
                        at_least(pool, C_loaded[u // C], 16 * (i + 1))
                    at_least(pool, h_ready, k + 1)
                    h = h_sb[:, u % RH, :]
                    nc.gpsimd.tensor_tensor(h, h, C_sb[:, u // C, :], ALU.mult).then_inc(hc_ready, 1)
                    if has_projection(g) and u == POOL_SLOT["store_B"]:
                        store_B(g + 1, j, i + G)
                    if has_projection(g) and u == POOL_SLOT["scale_x"]:
                        scale_x(g + 1, j, i + G)
                if g == 0:
                    at_least(pool, fsum_copied, j + 1)
                    diag = F_sb[:, :, :].rearrange("p c d -> p (c d)")
                    diag = diag[:, bass.ds(j * (D + P), P)] if not isinstance(j, int) else diag[:, j * (D + P):j * (D + P) + P]
                    nc.gpsimd.tensor_tensor(diag, diag, ident_sb[:, :], ALU.add).then_inc(F_ready, 1)

            run_iterations(pool, iteration)
            rstd(2, NT - G - 2)
            for t, place in last_tiles:
                rstd(0, t, place)
            rstd(1, *before_last)
            rstd(2, *before_last)
            for n in (1, 2):
                for t, place in last_tiles:
                    rstd(n, t, place)

        @block.scalar
        def _(act):
            nc.scalar.preload_act_table_set("natural_log_exp_and_others")
            for dst, src, loaded in ((raw_sb[:, :], bias_rows, biases_in), (blo_sb[:, :], b_lo, blo_in),
                                     (WdtT_sb[:, :], WdtT, Wdt_in), (bbc_sb[:, :], b_bc, bbc_in),
                                     (sel_raw[:, :], sel_rows, sel_in), (ident_sb[:, :], ident, ident_in),
                                     (D1_sb[:, :], Dv, Dv_in)):
                act.dma_start(dst, src).then_inc(loaded, 16)

            def copy_lo(t):
                at_least(act, lo_ready, t + 1)
                nc.scalar.activation(lo_sb[:, :], pj_ps[:, 0:R], ACT.Identity, bias=blo_sb[:, :])
                at_least(act, b_stored, t)
                nc.scalar.activation(bc_sb[:, :], pj_ps[:, R:R + 2 * S], ACT.Copy).then_inc(bc_copied, 1)

            def sp_abs(t):
                at_least(act, z_ready, t + 1)
                nc.scalar.activation(sp_sb[:, :], pj_ps[:, :], ACT.Abs).then_inc(abs_done, 1)

            def sp_exp(t):
                at_least(act, abs_done, t + 1)
                nc.scalar.activation(sp_sb[:, :], sp_sb[:, :], ACT.Exp, scale=-1.0).then_inc(spexp_done, 1)

            def sp_ln(t):
                at_least(act, spexp_done, t + 1)
                nc.scalar.activation(sp_sb[:, :], sp_sb[:, :], ACT.Ln, bias=1.0).then_inc(spln_done, 1)

            act.wait_ge(blo_in, 16)
            act.wait_ge(lo_ready, G)
            nc.scalar.activation(first_lo, bx_ps[:, 0, :], ACT.Identity, bias=blo_sb[:, :]).then_inc(bc_copied, G)
            act.wait_ge(alog_in, 16)
            nc.scalar.activation(A_sb[:, :, :], A_sb[:, :, :], ACT.Exp).then_inc(A_exp, 1)
            for step in range(G + 2):
                if step < G:
                    act.wait_ge(z_ready, step + 1)
                    nc.scalar.activation(first_sp(step), y_ps[:, step, :], ACT.Abs).then_inc(abs_done, 1)
                if 1 <= step <= G:
                    act.wait_ge(abs_done, step)
                    nc.scalar.activation(first_sp(step - 1), first_sp(step - 1), ACT.Exp, scale=-1.0
                                         ).then_inc(spexp_done, 1)
                if step >= 2:
                    act.wait_ge(spexp_done, step - 1)
                    nc.scalar.activation(first_sp(step - 2), first_sp(step - 2), ACT.Ln, bias=1.0
                                         ).then_inc(spln_done, 1)

            def product(half, n, q, b, slot_count):
                if b == 0:
                    at_least(act, bx_ready, slot_count)
                scale = B_sb[:, :, :, :].rearrange("p g s b -> p (g s b)")
                scale = scale[:, n * G + b:n * G + b + 1] if isinstance(n, int) else scale[:, bass.ds(n * G + b, 1)]
                src = dx_sb[:, half, b, :] if isinstance(half, int) else dx_sb[:, one(half), b, :].rearrange("p a d -> p (a d)")
                nc.scalar.activation(prod_sb[:, q, b, :], src, ACT.Copy, scale=scale).then_inc(prod_ready, 1)

            def flat(v):
                return v.rearrange("p c n -> p (c n)")

            def x1T_copy(t, place=lane):
                at_least(act, x1T_ready, t + 1)
                nc.scalar.activation(flat(place.x1T), place.bank, ACT.Copy).then_inc(x1T_copied, 1)

            def probs(t, place=lane):
                n = slice(place.n, place.n + 1)
                at_least(act, nmx_ready, t + 1)
                nc.scalar.activation(place.p, place.sc, ACT.Exp, bias=nmx_sb[:, n], accum_out=sum_sb[:, n]
                                     ).then_inc(p_ready, 1)

            def pT_copy(t, place=lane):
                at_least(act, pT_ready, t + 1)
                nc.scalar.activation(place.pT, place.bank[:, 0:P], ACT.Copy).then_inc(pT_copied, 1)

            def x2_norm(t, place=lane):
                at_least(act, nmr_ready, t + 1)
                nc.scalar.activation(place.x2, place.bank, ACT.Identity, bias=nmr_sb[:, place.n:place.n + 1],
                                     scale=rstd_sb[:, place.n, 1:2]).then_inc(x2_ready, 1)

            def x2T_copy(t, place=lane):
                at_least(act, x2T_ready, t + 1)
                nc.scalar.activation(flat(place.x2T), place.ffn_bank, ACT.Copy).then_inc(x2T_copied, 1)

            def z1_copy(g, b):
                at_least(act, y_added, GU * (g + 1))
                at_least(act, x1_ready, G * g)
                nc.scalar.activation(z1_sb[:, b, :], y_ps[:, b, :], ACT.Copy).then_inc(z1_by_act, 1)

            act.wait_ge(b_stored, G)
            for b in range(G):
                act.wait_ge(dx_ready, b + 1)
                product(0, 0, 0, b, 0)
            act.wait_ge(xd_ready, G)
            act.wait_ge(A_ready, 1)
            act.wait_ge(zeroed, 1)

            def iteration(g, j):
                i = IT * g + j
                tile = attention_tile(g, j)
                last = g == NG - 1 and isinstance(j, int) and j == IT - 1
                if isinstance(j, int) and j == 0:
                    if g == 0:
                        act.wait_ge(delta_ready, G)
                    else:
                        act.wait_ge(delta_stored, loads(G * (g + 1) - 1))
                for u in range(U):
                    k = U * i + u
                    q, c = u // C, u % C
                    at_least(act, h_ready, k - RA + 1)
                    s = Q * j + q
                    A_col = A_sb[:, c, s:s + 1] if isinstance(s, int) else A_sb[:, c, one(s)]
                    nc.scalar.activation(a_sb[:, u % RA, :, 1:], delta_sb[:, g % 2, c, :, 1:], ACT.Exp, scale=A_col
                                         ).then_inc(a_ready, 1)
                    if q < Q - 1:
                        product(g % 2, Q * i + q + 1, q + 1, c, U * (i - 1) + C * (q + 2))
                    elif not last:
                        if c == 0 and has_projection(g):
                            at_least(act, dx_ready, (i + 1) // IT * IT + G)
                            at_least(act, b_stored, (i + 1) // IT * IT + G)
                        half = ((i + 1) // IT) % 2 if isinstance(j, int) else (
                            (g % 2) if not has_projection(g) else (j + 1 + IT * g) // IT % 2)
                        product(half, Q * (i + 1), 0, c, U * i + C)
                    if has_projection(g):
                        if u == ACT_SLOT["copy_lo"]:
                            copy_lo(i + G)
                        if u == ACT_SLOT["sp_abs"]:
                            sp_abs(i + G)
                        if u == ACT_SLOT["sp_exp"]:
                            sp_exp(i + G)
                        if u == ACT_SLOT["sp_ln"]:
                            sp_ln(i + G)
                    if g == 0 and u == ACT_SLOT["F"]:
                        at_least(act, fac_added, (RANK - 1) * (j + 1))
                        nc.scalar.activation(F_sb[:, one(j), :].rearrange("p a d -> p (a d)"), fac_sb[:, 0, :],
                                             ACT.Copy, scale=FSCALE).then_inc(fsum_copied, 1)
                    if tile is not None:
                        if u == ACT_SLOT["x1T"]:
                            x1T_copy(tile)
                        if u == ACT_SLOT["probs"]:
                            probs(tile)
                        if u == ACT_SLOT["pT"]:
                            pT_copy(tile)
                        if u == ACT_SLOT["x2_norm"]:
                            x2_norm(tile)
                        if u == ACT_SLOT["x2T"]:
                            x2T_copy(tile)
                    if g > 0 and isinstance(j, int) and j == 0 and u == ACT_SLOT["z1"]:
                        z1_copy(g - 1, 2)
                        z1_copy(g - 1, 3)

            run_iterations(act, iteration)

            x1T_copy(*before_last)
            probs(*before_last)
            pT_copy(*before_last)
            for t, place in last_tiles:
                x1T_copy(t, place)
            x2_norm(*before_last)
            x2T_copy(*before_last)
            for step in (probs, pT_copy, x2_norm, x2T_copy):
                for t, place in last_tiles:
                    step(t, place)

        @block.tensor
        def _(pe):
            def transpose(dst, src, start=True):
                return nc.tensor.matmul(dst, src, ident_sb[:, :], start=start, stop=True, is_transpose=True,
                                        skip_group_check=True)

            def proj_bc(t, finished):
                at_least(pe, o_ready, finished)
                at_least(pe, xT_loaded, loads(t))
                at_least(pe, dx_ready, t)
                nc.tensor.matmul(pj_ps[:, R:R + 2 * S], ones_sb[:, :], biases_sb[:, D:D + 2 * S], start=True,
                                 stop=False)
                for c in range(C):
                    nc.tensor.matmul(pj_ps[:, R:R + 2 * S], xT_in[:, c, :], WdbcT_sb[:, c, R:R + 2 * S], start=False,
                                     stop=c == C - 1)

            def proj_lo(t):
                for c in range(C):
                    last = nc.tensor.matmul(pj_ps[:, 0:R], WdbcT_sb[:, c, 0:R], xT_in[:, c, :], start=c == 0,
                                            stop=c == C - 1)
                last.then_inc(lo_ready, 1)

            def proj_ct(t):
                at_least(pe, bc_copied, t + 1)
                transpose(pj_ps[0:S, 0:P], bc_sb[:, S:2 * S]).then_inc(ct_ready, 1)

            def proj_z(t, chunks):
                if 0 in chunks:
                    at_least(pe, ct_copied, t + 1)
                    nc.tensor.matmul(pj_ps[:, :], biases_sb[:, D + 2 * S:NB], sel_sb[:, :], start=True, stop=False,
                                     skip_group_check=True)
                for c in chunks:
                    last = nc.tensor.matmul(pj_ps[:, c * P:(c + 1) * P], WdtT_sb[:, c * P:(c + 1) * P], lo_sb[:, :],
                                            start=False, stop=c == C - 1, skip_group_check=True)
                if C - 1 in chunks:
                    last.then_inc(z_ready, 1)

            def proj_dT(t):
                at_least(pe, delta_ready, t + 1)
                for c in range(C):
                    last = transpose(pj_ps[:, c * P:(c + 1) * P], delta_t[:, c, :])
                last.then_inc(dT_ready, 1)

            pe.wait_ge(Wdbc_in, 16)
            def xT_chunk(c):
                return prod_sb[:, 1, :, c * P:(c + 1) * P]

            for c in range(C):
                pe.wait_ge(first_xT_in[c], 16)
                last = nc.tensor.matmul(bx_ps[:, 0, :], WdbcT_sb[:, c, 0:R], xT_chunk(c), start=c == 0, stop=c == C - 1)
            last.then_inc(lo_ready, G)
            for c in range(C):
                last = nc.tensor.matmul(bx_ps[0:2 * S, 1, :], WdbcT_sb[:, c, R:R + 2 * S], xT_chunk(c), start=c == 0,
                                        stop=c == C - 1)
            last.then_inc(ct_ready, G)
            pe.wait_ge(Wdt_in, 16)
            pe.wait_ge(bc_copied, G)
            for b in range(G):
                for c in range(C):
                    nc.tensor.matmul(y_ps[:, b, c * P:(c + 1) * P], WdtT_sb[:, c * P:(c + 1) * P],
                                     first_lo[:, b * P:(b + 1) * P], start=c == 0, stop=False, skip_group_check=True)
                if b == 0:
                    pe.wait_ge(biases_ready, PARTS)
                    pe.wait_ge(sel_ready, 1)
                nc.tensor.matmul(y_ps[:, b, :], biases_sb[:, D + 2 * S:NB], sel_sb[:, :], start=False, stop=True,
                                 skip_group_check=True).then_inc(z_ready, 1)
            pe.wait_ge(ones_ready, 1)
            pe.wait_ge(ident_in, 16)
            pe.wait_ge(ct_copied, G)
            for b in range(G):
                last = nc.tensor.matmul(at_ps[:, b * S:(b + 1) * S], first_bcT[0:S, b * P:(b + 1) * P], ident_sb[0:S, 0:S],
                                        start=True, stop=True, is_transpose=True, skip_group_check=True)
            last.then_inc(BT_ready, 1)
            for b in range(G):
                pe.wait_ge(delta_ready, b + 1)
                for c in range(C):
                    last = transpose(y_ps[:, b, c * P:(c + 1) * P], delta_sb[:, 0, c, b, :])
                last.then_inc(dT_ready, 1)

            def x1_transpose(t, place=lane):
                at_least(pe, x1_ready, t + 1)
                if place is lane:
                    at_least(pe, x2_ready, t)
                for c in range(C):
                    last = transpose(place.bank[:, c * P:(c + 1) * P], place.x1[:, c * P:(c + 1) * P])
                last.then_inc(x1T_ready, 1)

            def scores(t, place=lane):
                at_least(pe, x1T_copied, t + 1)
                if place is lane:
                    at_least(pe, ctxT_loaded, 16 * (t + 1))
                else:
                    pe.wait_ge(last_ctx_in, 32)
                for c in range(C):
                    last = nc.tensor.matmul(place.bank[:, 0:P], place.x1T[:, c, :], place.ctxT[:, c, :], start=c == 0,
                                            stop=c == C - 1)
                last.then_inc(scores_ready, 1)

            def p_transpose(t, place=lane):
                at_least(pe, pn_ready, t + 1)
                transpose(place.bank[:, 0:P], place.pn).then_inc(pT_ready, 1)

            def residual(t, place=lane):
                at_least(pe, pT_copied, t + 1)
                for c in range(C):
                    transpose(place.bank[:, c * P:(c + 1) * P], place.x1T[:, c, :], start=c == 0)

            def readout(t, place=lane):
                if place is lane:
                    at_least(pe, ctx_loaded, 16 * (t + 1))
                nc.tensor.matmul(place.bank, place.pT, place.ctx, start=False, stop=True, skip_group_check=True
                                 ).then_inc(z2_ready, 1)

            def x2_transpose(t, projected, place=lane):
                at_least(pe, x2_ready, t + 1)
                if place is lane:
                    at_least(pe, dx_ready, projected)
                    at_least(pe, o_ready, t)
                for c in range(C):
                    last = transpose(place.ffn_bank[:, c * P:(c + 1) * P], place.x2[:, c * P:(c + 1) * P])
                last.then_inc(x2T_ready, 1)

            def ffn(t, c, place=lane):
                if c == 0:
                    pe.wait_ge(F_ready, C)
                    at_least(pe, x2T_copied, t + 1)
                    nc.tensor.matmul(place.ffn_bank, ones_sb[:, :], biases_sb[:, 0:D], start=True, stop=False)
                last = nc.tensor.matmul(place.ffn_bank, place.x2T[:, c, :], F_sb[:, c, :], start=False,
                                        stop=c == C - 1)
                if c == C - 1:
                    last.then_inc(z3_ready, 1)

            def unit_bx(g, j, u):
                i = IT * g + j
                q, c = u // C, u % C
                if c == 0:
                    at_least(pe, prod_ready, G * (Q * i + q + 1))
                at_least(pe, h_ready, U * i + u - 1)
                for b in range(G):
                    last = transpose(bx_ps[:, u % 2, b * P:(b + 1) * P], prod_sb[:, q, b, c * P:(c + 1) * P])
                last.then_inc(bx_ready, 1)

            def unit_y(k, u):
                at_least(pe, hc_ready, k + 1)
                c = u % C
                for b in range(G):
                    last = transpose(y_ps[:, b, c * P:(c + 1) * P], h_sb[:, u % RH, b * P:(b + 1) * P], start=False)
                last.then_inc(y_added, 1)

            def skip(g):
                at_least(pe, z1_by_dve, 2 * g)
                at_least(pe, z1_by_act, 2 * g)
                at_least(pe, xd_ready, G * (g + 1))
                for b in range(G):
                    for c in range(C):
                        last = transpose(y_ps[:, b, c * P:(c + 1) * P], xd_sb[:, b, c, :], start=c == 0)
                last.then_inc(skip_added, 1)

            def iteration(g, j):
                i = IT * g + j
                tile = attention_tile(g, j)
                for u in range(U):
                    unit_bx(g, j, u)
                    k = U * i + u - LAG
                    if isinstance(j, int) and j == 0 and u == LAG:
                        skip(g)
                    if not (isinstance(k, int) and k < 0):
                        unit_y(k, (u - LAG) % U)
                    if has_projection(g):
                        if u == PE_SLOT["bc"]:
                            proj_bc(i + G, 0 if tile is None else tile)
                        if u == PE_SLOT["lo"]:
                            proj_lo(i + G)
                        if u == PE_SLOT["ct"]:
                            proj_ct(i + G)
                        if u == PE_SLOT["z"][0]:
                            proj_z(i + G, range(C // 2))
                        if u == PE_SLOT["z"][1]:
                            proj_z(i + G, range(C // 2, C))
                        if u == PE_SLOT["dT"]:
                            proj_dT(i + G)
                    if tile is not None:
                        if u == PE_SLOT["scores"]:
                            scores(tile)
                        if u == PE_SLOT["pT"]:
                            p_transpose(tile)
                        if u == PE_SLOT["residual"]:
                            residual(tile)
                        if u == PE_SLOT["readout"]:
                            readout(tile)
                        if u == PE_SLOT["x2T"]:
                            x2_transpose(tile, i + G + 1 if has_projection(g) else NT)
                        for c in range(C):
                            if u == PE_SLOT["ffn"][c]:
                                ffn(tile, c)
                    if prepares_x1(g) and u == PE_SLOT["x1T"]:
                        x1_transpose(i - G)

            run_iterations(pe, iteration)
            scores(*before_last)
            for u in range(U - LAG, U):
                if u == U - 1:
                    p_transpose(*before_last)
                unit_y(GU * NG - U + u, u)
            residual(*before_last)
            readout(*before_last)
            for t, place in last_tiles:
                x1_transpose(t, place)
            for n, (t, place) in enumerate(last_tiles):
                scores(t, place)
                if n == 1:
                    x2_transpose(NT - G - 1, NT)
            for c in range(C):
                ffn(NT - G - 1, c)
            for t, place in last_tiles:
                p_transpose(t, place)
            for t, place in last_tiles:
                residual(t, place)
                readout(t, place)
            for t, place in last_tiles:
                x2_transpose(t, NT, place)
            for t, place in last_tiles:
                for c in range(C):
                    ffn(t, c, place)

        @block.vector
        def _(dve):
            nc.vector.memset(a_sb[:, :, :, 0:1], 0.0).then_inc(zeroed, 1)
            dve.wait_ge(biases_in, 16)
            for part in range(PARTS):
                rest = raw_sb if part == 0 else rest_sb
                nc.vector.tensor_copy(part_sb[:, :], rest[:, :]).then_inc(bias_step, 1)
                dve.wait_ge(bias_step, 2 * part + 1)
                rows = slice(32 * part, 32 * part + 32)
                nc.vector.tensor_copy(biases_sb[rows, :], part_sb[rows, :]).then_inc(biases_ready, 1)
                if part < PARTS - 1:
                    nc.vector.tensor_tensor(rest_sb[:, :], rest[:, :], part_sb[:, :], ALU.subtract
                                            ).then_inc(bias_step, 1)
                    dve.wait_ge(bias_step, 2 * part + 2)
                    dve.wait_ge(biases_ready, part + 1)
            dve.wait_ge(sel_in, 16)
            nc.vector.tensor_copy(sel_sb[:, :], sel_raw[:, :]).then_inc(sel_ready, 1)
            dve.wait_ge(Dv_in, 16)
            nc.vector.tensor_scalar(D1_sb[:, :], D1_sb[:, :], 1.0, None, ALU.add).then_inc(D1_ready, 1)

            def expand_mask():
                dve.wait_ge(mask_in, 16)
                nc.vector.tensor_scalar(neg_sb[:, :], mask_sb[:, :], BIG, BIG, ALU.mult, ALU.subtract
                                        ).then_inc(neg_ready, 1)
                dve.wait_ge(neg_ready, 1)
                nc.vector.reduce_max(best_sb[:, :], neg_sb[:, :].rearrange("p (b n) -> p b n", n=P), AX_X
                                     ).then_inc(best_ready, 1)
                dve.wait_ge(best_ready, 1)
                nc.vector.tensor_scalar(valid_sb[:, :], best_sb[:, :], 0.0, None, ALU.is_ge).then_inc(valid_ready, 1)
                dve.wait_ge(valid_ready, 1)

            def copy_ct(t):
                at_least(dve, ct_ready, t + 1)
                at_least(dve, ct_stored, loads(t))
                nc.vector.tensor_copy(ct_sb[:, :], pj_ps[0:S, 0:P]).then_inc(ct_copied, 1)

            def softplus_end(t):
                at_least(dve, spln_done, t + 1)
                at_least(dve, delta_stored, loads(t - 1))
                nc.vector.scalar_tensor_tensor(delta_t[:, :, :].rearrange("p c n -> p (c n)"), pj_ps[:, :], 0.0,
                                               sp_sb[:, :], ALU.max, ALU.add).then_inc(delta_ready, 1)

            def delta_x(g, tile, t):
                at_least(dve, dT_ready, t + 1)
                at_least(dve, x_loaded, loads(t))
                at_least(dve, prod_ready, G * S * (g - 1))
                nc.vector.tensor_tensor(dx_sb[:, g % 2, one(tile), :].rearrange("p a d -> p (a d)"), pj_ps[:, :],
                                        x_in[:, :], ALU.mult).then_inc(dx_ready, 1)

            dve.wait_ge(ct_ready, G)
            dve.wait_ge(bbc_in, 16)
            nc.vector.tensor_scalar(first_bcT, bx_ps[0:2 * S, 1, :], bbc_sb[:, :], None, ALU.add).then_inc(ct_copied, G)
            dve.wait_ge(A_exp, 1)
            nc.vector.tensor_scalar(A_sb[:, :, :], A_sb[:, :, :], -1.0, None, ALU.mult).then_inc(A_ready, 1)
            dve.wait_ge(BT_ready, 1)
            nc.vector.tensor_copy(B_sb[:, 0, :, :], at_ps[:, 0:G * S].rearrange("p (b s) -> p s b", s=S)
                                  ).then_inc(b_stored, G)
            for b in range(G):
                dve.wait_ge(spln_done, b + 1)
                nc.vector.scalar_tensor_tensor(delta_sb[:, 0, :, b, :], y_ps[:, b, :].rearrange("p (c n) -> p c n", n=P),
                                               0.0, first_sp(b).rearrange("p (c n) -> p c n", n=P), ALU.max, ALU.add
                                               ).then_inc(delta_ready, 1)
            dve.wait_ge(first_x_in, 16)
            for b in range(G):
                dve.wait_ge(dT_ready, b + 1)
                nc.vector.tensor_tensor(dx_sb[:, 0, b, :], y_ps[:, b, :], first_x(b), ALU.mult).then_inc(dx_ready, 1)

            def stats(n, tiles):
                for t, column, src in tiles:
                    nc.vector.bn_stats(st_sb[:, column, n, :], src).then_inc(st_done[n], 1)
                for t, column, src in tiles:
                    at_least_alone(dve, st_done[n], t + 1)
                    nc.vector.bn_aggr(mv_sb[:, column, n, :], st_sb[:, column, n, :]).then_inc(mv_done[n], 1)
                for t, column, src in tiles:
                    at_least(dve, mv_done[n], t + 1)
                    nc.vector.tensor_scalar(ve_sb[:, column, n:n + 1], mv_sb[:, column, n, 1:2], EPS, None, ALU.add
                                            ).then_inc(ve_done[n], 1)

            def z1_stats(t, place):
                stats(0, [(t, 0, z1_sb[:, one(place), :].rearrange("p a d -> p (a d)"))])

            def x1_norm(t, z1, place):
                at_least(dve, rstd_done[0], t + 1)
                nc.vector.tensor_scalar(place.x1, z1, mv_sb[:, place.n, 0, 0:1], rstd_sb[:, place.n, 0:1],
                                        ALU.subtract, ALU.mult).then_inc(x1_ready, 1)

            def mask_and_max(t, place=lane):
                n = slice(place.n, place.n + 1)
                at_least(dve, scores_ready, t + 1)
                neg = neg_sb[:, t * P:(t + 1) * P] if isinstance(t, int) else neg_sb[:, bass.ds(t * P, P)]
                nc.vector.scalar_tensor_tensor(place.sc, place.bank[:, 0:P], SCALE, neg, ALU.mult, ALU.add
                                               ).then_inc(masked, 1)
                at_least(dve, masked, t + 1)
                nc.vector.reduce_max(mx_sb[:, n], place.sc, AX_X).then_inc(max_done, 1)
                at_least(dve, max_done, t + 1)
                nc.vector.tensor_scalar(nmx_sb[:, n], mx_sb[:, n], -1.0, None, ALU.mult).then_inc(nmx_ready, 1)

            def normalise_probs(t, place=lane):
                n = slice(place.n, place.n + 1)
                at_least(dve, p_ready, t + 1)
                nc.vector.reciprocal(rs_sb[:, n], sum_sb[:, n]).then_inc(rs_done, 1)
                at_least(dve, rs_done, t + 1)
                nc.vector.tensor_tensor(rv_sb[:, n], rs_sb[:, n], valid_sb[:, one(t)], ALU.mult).then_inc(rv_done, 1)
                at_least(dve, rv_done, t + 1)
                nc.vector.tensor_scalar(place.pn, place.p, rv_sb[:, n], None, ALU.mult).then_inc(pn_ready, 1)

            def z2_stats(t, place=lane):
                at_least(dve, z2_ready, t + 1)
                stats(1, [(t, place.n, place.bank)])

            def z2_shift(t, place=lane):
                at_least(dve, rstd_done[1], t + 1)
                nc.vector.scalar_tensor_tensor(nmr_sb[:, place.n:place.n + 1], mv_sb[:, place.n, 1, 0:1], -1.0,
                                               rstd_sb[:, place.n, 1:2], ALU.mult, ALU.mult).then_inc(nmr_ready, 1)

            def z3_stats(t, place=lane):
                at_least(dve, z3_ready, t + 1)
                stats(2, [(t, place.n, place.ffn_bank)])

            def z3_norm(t, place=lane):
                at_least(dve, rstd_done[2], t + 1)
                if place is lane:
                    at_least(dve, out_stored, 16 * t)
                nc.vector.tensor_scalar(place.o, place.ffn_bank, mv_sb[:, place.n, 2, 0:1], rstd_sb[:, place.n, 2:3],
                                        ALU.subtract, ALU.mult).then_inc(o_ready, 1)

            def z1_copy(g, b):
                at_least(dve, y_added, GU * (g + 1))
                at_least(dve, x1_ready, G * g)
                nc.vector.tensor_copy(z1_sb[:, b, :], y_ps[:, b, :]).then_inc(z1_by_dve, 1)

            pairs = [(r, r + n) for n in (4, 2, 1) for r in range(n)]

            def add_factor(j, step):
                r, other = pairs[step]
                if step == 0:
                    at_least(dve, fac_loaded, 16 * (j + 1))
                if step >= RANK // 2:
                    at_least(dve, fac_added, (RANK - 1) * j + step)
                nc.vector.tensor_tensor(fac_sb[:, r, :], fac_sb[:, r, :], fac_sb[:, other, :], ALU.add
                                        ).then_inc(fac_added, 1)

            def iteration(g, j):
                i = IT * g + j
                tile = attention_tile(g, j)
                for u in range(U):
                    k = U * i + u
                    at_least(dve, a_ready, k + 1)
                    at_least(dve, bx_ready, k + 1)
                    at_least(dve, y_added, k - RH + 1)
                    nc.vector.tensor_tensor_scan(h_sb[:, u % RH, :], a_sb[:, u % RA, :, :].rearrange("p b n -> p (b n)"),
                                                 bx_ps[:, u % 2, :], 0.0, ALU.mult, ALU.add).then_inc(h_ready, 1)
                    if g == 0 and isinstance(j, int) and u == LAG:
                        expand_mask()
                    if g == 0 and FACTOR_SLOT <= u < FACTOR_SLOT + RANK - 1:
                        add_factor(j, u - FACTOR_SLOT)
                    if has_projection(g):
                        if u == DVE_SLOT["copy_ct"]:
                            copy_ct(i + G)
                        if u == DVE_SLOT["softplus_end"]:
                            softplus_end(i + G)
                        if u == DVE_SLOT["delta_x"]:
                            delta_x(g + 1, j, i + G)
                    if tile is not None:
                        if u == DVE_SLOT["z3_norm"] and finishes_tile(g, j):
                            z3_norm(tile - 1)
                        if u == DVE_SLOT["mask"]:
                            mask_and_max(tile)
                        if u == DVE_SLOT["normalise"]:
                            normalise_probs(tile)
                        if u == DVE_SLOT["z2_stats"]:
                            z2_stats(tile)
                        if u == DVE_SLOT["z2_shift"]:
                            z2_shift(tile)
                        if u == DVE_SLOT["z3_stats"]:
                            z3_stats(tile)
                    if prepares_x1(g):
                        if u == DVE_SLOT["z1_stats"]:
                            if isinstance(j, int) and j == 0:
                                dve.wait_ge(z1_by_act, 2 * g)
                                dve.wait_ge(z1_by_dve, 2 * g)
                            z1_stats(i - G, j)
                        if u == DVE_SLOT["x1_norm"]:
                            x1_norm(i - G, z1_sb[:, one(j), :].rearrange("p a d -> p (a d)"), lane)
                    if g > 0 and isinstance(j, int) and j == 0 and u == LAG - 1:
                        z1_copy(g - 1, 0)
                        z1_copy(g - 1, 1)

            run_iterations(dve, iteration)

            mask_and_max(*before_last)
            normalise_probs(*before_last)
            z3_norm(NT - G - 2)
            dve.wait_ge(y_added, GU * NG)
            stats(0, [(t, place.n, place.bank) for t, place in last_tiles])
            z2_stats(*before_last)
            for t, place in last_tiles:
                x1_norm(t, place.bank, place)
            z2_shift(*before_last)
            for t, place in last_tiles:
                mask_and_max(t, place)
            for t, place in last_tiles:
                normalise_probs(t, place)
            z3_stats(*before_last)
            for t, place in last_tiles:
                z2_stats(t, place)
                if place is last_lanes[0]:
                    z3_norm(*before_last)
                else:
                    z2_shift(t - 1, last_lanes[place.n - 2])
            z2_shift(*last_tiles[-1])
            for t, place in last_tiles:
                z3_stats(t, place)
                z3_norm(t, place)


def kernel(x, ctx_2048, mask_BxS2_bk0, L0_attn_W_dbc, L0_attn_b_dbc, L0_attn_W_dt, L0_attn_b_dt, L0_attn_A_log,
           L0_attn_D, L0_ffn_factors, L0_ffn_bias):
    import numpy as np
    import concourse.bacc as bacc
    from concourse import mybir as mb
    from concourse.bass_utils import run_bass_kernel_spmd

    def channels_first(v):
        v = np.asarray(v).transpose(0, 2, 1).reshape(NT, C, P, P)
        return np.ascontiguousarray(v.transpose(0, 2, 1, 3))

    def quadrants(*blocks):
        rows = np.zeros((KB, sum(v.shape[1] for v in blocks)), np.float32)
        for first in range(0, KB, 32):
            column = 0
            for v in blocks:
                rows[first:first + v.shape[0], column:column + v.shape[1]] = v
                column += v.shape[1]
        return rows

    b_dbc = np.asarray(L0_attn_b_dbc)
    arrays = {
        "x": np.asarray(x),
        "xT": channels_first(x),
        "ctx": np.asarray(ctx_2048),
        "ctxT": channels_first(ctx_2048),
        "mask": np.asarray(mask_BxS2_bk0).reshape(1, NT * P),
        "WdbcT": np.ascontiguousarray(np.asarray(L0_attn_W_dbc).T),
        "b_lo": np.ascontiguousarray(b_dbc[:R].reshape(P, 1)),
        "b_bc": np.ascontiguousarray(b_dbc[R:].reshape(2 * S, 1)),
        "bias_rows": quadrants(np.concatenate([np.asarray(L0_ffn_bias), b_dbc[R:]]).reshape(1, D + 2 * S),
                               np.asarray(L0_attn_b_dt).reshape(C, P)),
        "WdtT": np.ascontiguousarray(np.asarray(L0_attn_W_dt).T),
        "A_log": np.asarray(L0_attn_A_log),
        "Dv": np.ascontiguousarray(np.asarray(L0_attn_D).reshape(C, P).T),
        "factors": np.asarray(L0_ffn_factors),
        "ident": np.eye(P, dtype=np.float32),
        "sel_rows": quadrants(np.repeat(np.eye(C, dtype=np.float32), P, axis=1)),
    }
    nc = bacc.Bacc("TRN2", target_bir_lowering=False, num_devices=1)
    args = {n: nc.dram_tensor(f"in_{n}", v.shape, mb.dt.from_np(v.dtype), kind="ExternalInput").ap()
            for n, v in arrays.items()}
    cT = nc.dram_tensor("c_spread", (NG, S, G, P), F32, kind="Internal").ap()
    out = nc.dram_tensor("out", (NT, P, D), F32, kind="ExternalOutput").ap()
    decoder_layer(nc, cT=cT, out=out, **args)
    r = run_bass_kernel_spmd(nc, [{f"in_{n}": v for n, v in arrays.items()}], core_ids=[0])
    return r.results[0]["out"]
```

```python
from collections import namedtuple
from contextlib import ExitStack

import concourse.bass as bass
from concourse import mybir

F32 = mybir.dt.float32
BF16 = mybir.dt.bfloat16
U8 = mybir.dt.uint8
ACT = mybir.ActivationFunctionType
ALU = mybir.AluOpType
AX_X = mybir.AxisListType.X

P = 128
NT = 16
D = 512
C = D // P
S = 16
R = 128
RANK = 8
G = 4
NG = NT // G
W = G * P
Q = 4
U = Q * C
IT = S // Q
GU = S * C
RA = 8
RH = 8
LAG = 5
TURN = 1
PARTS = 3
KB = 32 * PARTS
NB = D + 2 * S + P
PE_SLOT = dict(bc=1, lo=1, ct=2, z=(5, 6), dT=10, residual=1, readout=3, x2T=7, ffn=(8, 9, 10, 10), x1T=10,
               scores=12, pT=15)
DVE_SLOT = dict(copy_ct=3, softplus_end=8, delta_x=9, z2_stats=3, z2_mean=3, z2_shift=4, z3_stats=10,
                z3_mean=10, z3_norm=12, z1_stats=5, z1_mean=6, x1_norm=8, mask=12, normalise=14)
ACT_SLOT = dict(copy_lo=5, sp_abs=10, sp_exp=10, sp_ln=10, probs=0, pT=2, x2_norm=8, x2T=9, x1T=14, F=11,
                z1=7)
POOL_SLOT = dict(rstd0=8, rstd1=3, rstd2=11, store_B=3, scale_x=5)
FACTOR_SLOT = 2
EPS = 1e-5
BIG = 1e30
SCALE = float(D) ** -0.5
FSCALE = float(RANK) ** -0.5


Lane = namedtuple("Lane", "n front_bank bank x1 x1T ctx ctxT sc p pn pT x2 x2T o")


def at_least(eng, sem, value):
    if isinstance(value, int) and value <= 0:
        return
    eng.wait_ge(sem, value)


def one(i):
    return bass.ds(i, 1)


def decoder_layer(nc, x, xT, ctx, ctxT, mask, WdbcT, b_lo, b_bc, bias_rows, WdtT, A_log, Dv, factors, ident, sel_rows,
                  cT, out):
    with ExitStack() as stack:
        def sb(name, *shape, dt=F32):
            return stack.enter_context(nc.sbuf_tensor(name, list(shape), dt))

        def ps(name, *shape):
            return stack.enter_context(nc.psum_tensor(name, list(shape), F32))

        def sem(name):
            return stack.enter_context(nc.semaphore(name))

        ident_sb = sb("ident_sb", P, P)
        sel_raw = sb("sel_raw", KB, D)
        sel_sb = sb("sel_sb", KB, D, dt=BF16)
        WdbcT_sb = sb("WdbcT_sb", P, C, R + 2 * S)
        WdtT_sb = sb("WdtT_sb", P, D)
        blo_sb = sb("blo_sb", P, 1)
        bbc_sb = sb("bbc_sb", 2 * S, 1)
        A_sb = sb("A_sb", P, C, S)
        D1_sb = sb("D1_sb", P, C)
        raw_sb = sb("raw_sb", KB, NB)
        rest_sb = sb("rest_sb", KB, NB)
        part_sb = sb("part_sb", KB, NB, dt=BF16)
        biases_sb = sb("biases_sb", KB, NB, dt=BF16)
        ones_sb = sb("ones_sb", KB, P, dt=BF16)
        mhalf_sb = sb("mhalf_sb", P, 1)
        mask_sb = sb("mask_sb", P, NT * P, dt=U8)
        neg_sb = sb("neg_sb", P, NT * P)
        best_sb = sb("best_sb", P, NT)
        valid_sb = sb("valid_sb", P, NT)
        F_sb = sb("F_sb", P, C, D)
        fac_sb = sb("fac_sb", P, RANK, D)
        x_in = sb("x_in", P, D)
        xT_in = sb("xT_in", P, C, P)
        xd_sb = sb("xd_sb", P, G, C, P)
        lo_sb = sb("lo_sb", P, P)
        bc_sb = sb("bc_sb", P, 2 * S)
        ct_sb = sb("ct_sb", S, P)
        sp_sb = sb("sp_sb", P, D)
        delta_t = sb("delta_t", P, C, P)
        delta_sb = sb("delta_sb", P, 2, C, G, P)
        dx_sb = sb("dx_sb", P, 2, G, D)
        B_sb = sb("B_sb", P, NG, S, G)
        C_sb = sb("C_sb", P, Q, W)
        prod_sb = sb("prod_sb", P, Q, G, D)
        a_sb = sb("a_sb", P, RA, G, P)
        h_sb = sb("h_sb", P, RH, W)
        z1_sb = sb("z1_sb", P, G, D)
        x1_sb = sb("x1_sb", P, D)
        x1T_sb = sb("x1T_sb", P, C, P)
        ctx_in = sb("ctx_in", P, D)
        ctxT_in = sb("ctxT_in", P, C, P)
        sc_sb = sb("sc_sb", P, P)
        p_sb = sb("p_sb", P, P)
        pn_sb = sb("pn_sb", P, P)
        pT_sb = sb("pT_sb", P, P)
        x2_sb = sb("x2_sb", P, D)
        x2T_sb = sb("x2T_sb", P, C, P)
        o_sb = sb("o_sb", P, D)
        st_sb = sb("st_sb", P, G + 1, 3, 6)
        mv_sb = sb("mv_sb", P, G + 1, 3, 2)
        ve_sb = sb("ve_sb", P, G + 1, 3)
        rstd_sb = sb("rstd_sb", P, G + 1, 3)
        nmr_sb = sb("nmr_sb", P, G + 1)
        mx_sb = sb("mx_sb", P, G + 1)
        nmx_sb = sb("nmx_sb", P, G + 1)
        sum_sb = sb("sum_sb", P, G + 1)
        rs_sb = sb("rs_sb", P, G + 1)
        rv_sb = sb("rv_sb", P, G + 1)

        def first_xT(b):
            return prod_sb[:, 1, b, :].rearrange("p (c n) -> p c n", n=P)

        def first_x(b):
            return prod_sb[:, 2, b, :]

        def first_sp(b):
            return prod_sb[:, 3, b, :]

        first_lo = h_sb[:, 0, :]
        first_bcT = C_sb[0:2 * S, Q - 1, :]

        bx_ps = ps("bx_ps", P, 2, W)
        y_ps = ps("y_ps", P, G, D)
        pj_ps = ps("pj_ps", P, D)
        at_ps = ps("at_ps", P, D)

        def in_chunks(v):
            return v.rearrange("p (c n) -> p c n", n=P)

        lane = Lane(n=0, front_bank=pj_ps[:, :], bank=at_ps[:, :], x1=x1_sb[:, :], x1T=x1T_sb[:, :, :],
                    ctx=ctx_in[:, :], ctxT=ctxT_in[:, :, :], sc=sc_sb[:, :], p=p_sb[:, :], pn=pn_sb[:, :], pT=pT_sb[:, :], x2=x2_sb[:, :],
                    x2T=x2T_sb[:, :, :], o=o_sb[:, :])
        last_lanes = [Lane(n=b + 1, front_bank=y_ps[:, b, :], bank=y_ps[:, b, :], x1=prod_sb[:, 0, b, :],
                           x1T=in_chunks(prod_sb[:, 1, b, :]), ctx=fac_sb[:, b, :], ctxT=in_chunks(fac_sb[:, G + b, :]),
                           sc=a_sb[:, 0, b, :], p=a_sb[:, 1, b, :], pn=a_sb[:, 2, b, :], pT=a_sb[:, 3, b, :],
                           x2=prod_sb[:, 2, b, :], x2T=in_chunks(prod_sb[:, 3, b, :]), o=h_sb[:, b, :])
                      for b in range(G)]
        before_last = (NT - G - 1, lane)
        last_tiles = [(NT - G + b, last_lanes[b]) for b in range(G)]

        Wdbc_in, Wdt_in, blo_in, ident_in, Dv_in, alog_in, mask_in, x_loaded, xT_loaded = map(
            sem, ("Wdbc_in", "Wdt_in", "blo_in", "ident_in", "Dv_in", "alog_in", "mask_in", "x_loaded",
                  "xT_loaded"))
        first_xT_in = [sem(f"first_xT{c}_in") for c in range(C)]
        first_x_in, bbc_in, sel_in, BT_ready = map(sem, ("first_x_in", "bbc_in", "sel_in", "BT_ready"))
        ctx_loaded, ctxT_loaded, fac_loaded = map(sem, ("ctx_loaded", "ctxT_loaded", "fac_loaded"))
        last_ctx_in = sem("last_ctx_in")
        C_loaded = [sem(f"C{q}_loaded") for q in range(Q)]
        ct_stored, delta_stored, out_stored = map(sem, ("ct_stored", "delta_stored", "out_stored"))
        zeroed, A_exp, A_ready, D1_ready, neg_ready, best_ready, valid_ready, ones_ready, mhalf_ready, sel_ready = map(
            sem, ("zeroed", "A_exp", "A_ready", "D1_ready", "neg_ready", "best_ready", "valid_ready", "ones_ready",
                  "mhalf_ready", "sel_ready"))
        biases_in, bias_step, biases_ready = map(sem, ("biases_in", "bias_step", "biases_ready"))
        fac_added, fsum_copied, F_ready = map(sem, ("fac_added", "fsum_copied", "F_ready"))
        lo_ready, bc_copied, b_stored, ct_ready, ct_copied, z_ready = map(
            sem, ("lo_ready", "bc_copied", "b_stored", "ct_ready", "ct_copied", "z_ready"))
        abs_done, spexp_done, spln_done, delta_ready, dT_ready, dx_ready, xd_ready = map(
            sem, ("abs_done", "spexp_done", "spln_done", "delta_ready", "dT_ready", "dx_ready", "xd_ready"))
        prod_ready, a_ready, bx_ready, h_ready, hc_ready, y_added = map(
            sem, ("prod_ready", "a_ready", "bx_ready", "h_ready", "hc_ready", "y_added"))
        skip_added, z1_by_dve, z1_by_act = map(sem, ("skip_added", "z1_by_dve", "z1_by_act"))
        st_done = [sem(f"st{n}_done") for n in range(3)]
        mv_done = [sem(f"mv{n}_done") for n in range(3)]
        ve_done = [sem(f"ve{n}_done") for n in range(3)]
        rstd_done = [sem(f"rstd{n}_done") for n in range(3)]
        x1_ready, x1T_ready, x1T_copied, scores_ready, masked, max_done, nmx_ready, p_ready = map(
            sem, ("x1_ready", "x1T_ready", "x1T_copied", "scores_ready", "masked", "max_done", "nmx_ready",
                  "p_ready"))
        rs_done, rv_done, pn_ready, pT_ready, pT_copied, z2_ready, nmr_ready, x2_ready = map(
            sem, ("rs_done", "rv_done", "pn_ready", "pT_ready", "pT_copied", "z2_ready", "nmr_ready", "x2_ready"))
        x2T_ready, x2T_copied, z3_ready, o_ready = map(sem, ("x2T_ready", "x2T_copied", "z3_ready", "o_ready"))

        waits_carried = sem("waits_carried")

        def loads(t):
            return 16 * (t + 1 - G)

        def at_least_alone(eng, sem, value):
            at_least(eng, sem, value)
            if not isinstance(value, int):
                eng.sem_inc(waits_carried, 1)

        block = stack.enter_context(nc.Block())

        def run_iterations(eng, iteration):
            for g in range(NG):
                peeled = {0: (0,), 1: (0, 1)}.get(g, (0,))
                for j in peeled:
                    iteration(g, j)
                last = IT - 1 if g == NG - 1 else IT
                with eng.Fori(len(peeled), last) as j:
                    iteration(g, j)
                if g == NG - 1:
                    iteration(g, IT - 1)

        def has_projection(g):
            return g < NG - 1

        def prepares_x1(g):
            return g > 0

        def finished_tile(g, j):
            if g == 0 or (g == 1 and isinstance(j, int) and j == 0):
                return None
            return IT * g + j - G - 1

        @block.sync
        def _(sp):
            sp.dma_start(WdbcT_sb[:, :, :], WdbcT.rearrange("(c p) n -> p c n", p=P)).then_inc(Wdbc_in, 16)
            for c in range(C):
                sp.dma_start(prod_sb[:, 1, :, c * P:(c + 1) * P], xT[0:G, :, c, :].rearrange("b p n -> p b n")
                             ).then_inc(first_xT_in[c], 16)
            sp.dma_start(A_sb[:, :, :], A_log.rearrange("(c p) s -> p c s", p=P)).then_inc(alog_in, 16)
            sp.dma_start(prod_sb[:, 2, :, :], x[0:G, :, :].rearrange("b p d -> p b d")).then_inc(first_x_in, 16)
            sp.dma_start(mask_sb[:, :], mask.to_broadcast((P, NT * P))).then_inc(mask_in, 16)

            def load_tile(t):
                at_least_alone(sp, lo_ready, t)
                at_least_alone(sp, xd_ready, t)
                sp.dma_start(xT_in[:, :, :], xT[one(t), :, :, :].rearrange("a p c n -> p (a c) n")
                             ).then_inc(xT_loaded, 16)
                at_least_alone(sp, dx_ready, t)
                sp.dma_start(x_in[:, :], x[one(t), :, :].rearrange("a p d -> p (a d)")).then_inc(x_loaded, 16)

            def store_projection(g, tile, t):
                at_least_alone(sp, ct_copied, t + 1)
                sp.dma_start(cT[g, :, one(tile), :].rearrange("s a n -> s (a n)"), ct_sb[:, :]
                             ).then_inc(ct_stored, 16)

            def store_delta(g, tile, t):
                at_least_alone(sp, delta_ready, t + 1)
                at_least_alone(sp, a_ready, GU * (g - 1))
                sp.dma_start(delta_sb[:, g % 2, :, one(tile), :].rearrange("p c a n -> p c (a n)"),
                             delta_t[:, :, :]).then_inc(delta_stored, 16)

            def load_ctx(t):
                at_least_alone(sp, scores_ready, t)
                sp.dma_start(ctxT_in[:, :, :], ctxT[one(t), :, :, :].rearrange("a p c n -> p (a c) n")
                             ).then_inc(ctxT_loaded, 16)
                at_least_alone(sp, z2_ready, t)
                sp.dma_start(ctx_in[:, :], ctx[one(t), :, :].rearrange("a p d -> p (a d)")
                             ).then_inc(ctx_loaded, 16)

            def load_C(i, q, stored):
                at_least_alone(sp, ct_stored, loads(stored))
                at_least_alone(sp, hc_ready, U * (i - 1) + C * (q + 1))
                flat = cT.rearrange("g s b n -> (g s) (b n)")
                sp.dma_start(C_sb[:, q, :], flat[one(Q * i + q), :].to_broadcast((P, W))).then_inc(C_loaded[q], 16)

            sp.wait_ge(ct_copied, G)
            sp.dma_start(cT[0, :, :, :].rearrange("s b n -> s (b n)"), first_bcT[S:2 * S, :]).then_inc(ct_stored, 16)
            for q in range(Q - 1):
                load_C(0, q, G)

            def iteration(g, j):
                i = IT * g + j
                if has_projection(g):
                    load_tile(i + G)
                if g == 0:
                    at_least_alone(sp, fsum_copied, j)
                    rows = slice(j * P, (j + 1) * P) if isinstance(j, int) else bass.ds(j * P, P)
                    sp.dma_start(fac_sb[:, :, :], factors[:, rows, :].rearrange("r p e -> p r e")).then_inc(fac_loaded, 16)
                tile = finished_tile(g, j)
                if g == NG - 1 and isinstance(j, int) and j == 0:
                    sp.wait_ge(fsum_copied, C)
                    sp.dma_start(fac_sb[:, 0:G, :], ctx[NT - G:NT, :, :].rearrange("b p d -> p b d")
                                 ).then_inc(last_ctx_in, 16)
                    sp.dma_start(fac_sb[:, G:2 * G, :].rearrange("p b (c n) -> p b c n", n=P),
                                 ctxT[NT - G:NT, :, :, :].rearrange("b p c n -> p b c n")).then_inc(last_ctx_in, 16)
                if prepares_x1(g):
                    load_ctx(i - G)
                load_C(i, Q - 1, 0)
                if has_projection(g):
                    store_projection(g + 1, j, i + G)
                more = not (g == NG - 1 and isinstance(j, int) and j == IT - 1)
                if more:
                    load_C(i + 1, 0, i + G + 1 if has_projection(g) else NT)
                if has_projection(g):
                    store_delta(g + 1, j, i + G)
                for q in range(1, Q - 1):
                    if more:
                        load_C(i + 1, q, 0)
                if tile is not None:
                    store_out(tile, lane)

            def store_out(t, place):
                at_least_alone(sp, o_ready, t + 1)
                sp.dma_start(out[one(t), :, :].rearrange("a p d -> p (a d)"), place.o).then_inc(out_stored, 16)

            run_iterations(sp, iteration)

            for t, place in (before_last, *last_tiles):
                store_out(t, place)
            sp.wait_ge(out_stored, 16 * NT)

        @block.gpsimd
        def _(pool):
            nc.gpsimd.memset(ones_sb[:, :], 1.0).then_inc(ones_ready, 1)
            nc.gpsimd.memset(mhalf_sb[:, :], -0.5).then_inc(mhalf_ready, 1)
            pool.wait_ge(mhalf_ready, 1)

            def store_B(g, tile, t):
                at_least(pool, bc_copied, t + 1)
                nc.gpsimd.tensor_copy(B_sb[:, g, :, one(tile)].rearrange("p s a -> p (s a)"), bc_sb[:, 0:S]
                                      ).then_inc(b_stored, 1)

            def scale_x(g, tile, t):
                at_least(pool, xT_loaded, loads(t))
                at_least(pool, skip_added, g)
                nc.gpsimd.tensor_tensor(xd_sb[:, one(tile), :, :].rearrange("p a c n -> p (a c) n"), xT_in[:, :, :],
                                        D1_sb[:, :].rearrange("p (c a) -> p c a", a=1).to_broadcast((P, C, P)),
                                        ALU.mult).then_inc(xd_ready, 1)

            def rstd(n, t, place=lane):
                at_least(pool, ve_done[n], t + 1)
                nc.gpsimd.tensor_tensor(rstd_sb[:, place.n, n:n + 1], ve_sb[:, place.n, n:n + 1], mhalf_sb[:, :],
                                        ALU.pow).then_inc(rstd_done[n], 1)

            pool.wait_ge(D1_ready, 1)
            for c in range(C):
                pool.wait_ge(first_xT_in[c], 16)
            for b in range(G):
                nc.gpsimd.tensor_tensor(xd_sb[:, b, :, :], first_xT(b),
                                        D1_sb[:, :].rearrange("p (c a) -> p c a", a=1).to_broadcast((P, C, P)),
                                        ALU.mult).then_inc(xd_ready, 1)
            def iteration(g, j):
                i = IT * g + j
                tile = finished_tile(g, j)
                for u in range(U):
                    k = U * i + u
                    if tile is not None and u == POOL_SLOT["rstd2"]:
                        rstd(2, tile)
                    if tile is not None and u == POOL_SLOT["rstd1"]:
                        rstd(1, tile)
                    if prepares_x1(g) and u == POOL_SLOT["rstd0"]:
                        rstd(0, i - G)
                    if u % C == 0:
                        at_least(pool, C_loaded[u // C], 16 * (i + 1))
                    at_least(pool, h_ready, k + 1)
                    h = h_sb[:, u % RH, :]
                    nc.gpsimd.tensor_tensor(h, h, C_sb[:, u // C, :], ALU.mult).then_inc(hc_ready, 1)
                    if has_projection(g) and u == POOL_SLOT["store_B"]:
                        store_B(g + 1, j, i + G)
                    if has_projection(g) and u == POOL_SLOT["scale_x"]:
                        scale_x(g + 1, j, i + G)
                if g == 0:
                    at_least(pool, fsum_copied, j + 1)
                    diag = F_sb[:, :, :].rearrange("p c d -> p (c d)")
                    place = j * (D + P)
                    diag = diag[:, place:place + P] if isinstance(j, int) else diag[:, bass.ds(place, P)]
                    nc.gpsimd.tensor_tensor(diag, diag, ident_sb[:, :], ALU.add).then_inc(F_ready, 1)

            run_iterations(pool, iteration)
            rstd(1, *before_last)
            for t, place in last_tiles:
                rstd(0, t, place)
            rstd(2, *before_last)
            for n in (1, 2):
                for t, place in last_tiles:
                    rstd(n, t, place)

        @block.scalar
        def _(act):
            nc.scalar.preload_act_table_set("natural_log_exp_and_others")
            for dst, src, loaded in ((raw_sb[:, :], bias_rows, biases_in), (blo_sb[:, :], b_lo, blo_in),
                                     (WdtT_sb[:, :], WdtT, Wdt_in), (bbc_sb[:, :], b_bc, bbc_in),
                                     (sel_raw[:, :], sel_rows, sel_in), (ident_sb[:, :], ident, ident_in),
                                     (D1_sb[:, :], Dv, Dv_in)):
                act.dma_start(dst, src).then_inc(loaded, 16)

            def copy_lo(t):
                at_least(act, lo_ready, t + 1)
                nc.scalar.activation(lo_sb[:, :], pj_ps[:, 0:R], ACT.Identity, bias=blo_sb[:, :])
                at_least(act, b_stored, t)
                nc.scalar.activation(bc_sb[:, :], pj_ps[:, R:R + 2 * S], ACT.Copy).then_inc(bc_copied, 1)

            def sp_abs(t):
                at_least(act, z_ready, t + 1)
                nc.scalar.activation(sp_sb[:, :], pj_ps[:, :], ACT.Abs).then_inc(abs_done, 1)

            def sp_exp(t):
                at_least(act, abs_done, t + 1)
                nc.scalar.activation(sp_sb[:, :], sp_sb[:, :], ACT.Exp, scale=-1.0).then_inc(spexp_done, 1)

            def sp_ln(t):
                at_least(act, spexp_done, t + 1)
                nc.scalar.activation(sp_sb[:, :], sp_sb[:, :], ACT.Ln, bias=1.0).then_inc(spln_done, 1)

            act.wait_ge(blo_in, 16)
            act.wait_ge(lo_ready, G)
            nc.scalar.activation(first_lo, bx_ps[:, 0, :], ACT.Identity, bias=blo_sb[:, :]).then_inc(bc_copied, G)
            act.wait_ge(alog_in, 16)
            nc.scalar.activation(A_sb[:, :, :], A_sb[:, :, :], ACT.Exp).then_inc(A_exp, 1)
            for step in range(G + 2):
                if step < G:
                    act.wait_ge(z_ready, step + 1)
                    nc.scalar.activation(first_sp(step), y_ps[:, step, :], ACT.Abs).then_inc(abs_done, 1)
                if 1 <= step <= G:
                    act.wait_ge(abs_done, step)
                    nc.scalar.activation(first_sp(step - 1), first_sp(step - 1), ACT.Exp, scale=-1.0
                                         ).then_inc(spexp_done, 1)
                if step >= 2:
                    act.wait_ge(spexp_done, step - 1)
                    nc.scalar.activation(first_sp(step - 2), first_sp(step - 2), ACT.Ln, bias=1.0
                                         ).then_inc(spln_done, 1)

            def product(half, n, q, b, slot_count):
                if b == 0:
                    at_least(act, bx_ready, slot_count)
                scale = B_sb[:, :, :, :].rearrange("p g s b -> p (g s b)")
                scale = scale[:, n * G + b:n * G + b + 1] if isinstance(n, int) else scale[:, bass.ds(n * G + b, 1)]
                src = dx_sb[:, half if isinstance(half, int) else one(half), b, :]
                if not isinstance(half, int):
                    src = src.rearrange("p a d -> p (a d)")
                nc.scalar.activation(prod_sb[:, q, b, :], src, ACT.Copy, scale=scale).then_inc(prod_ready, 1)

            def flat(v):
                return v.rearrange("p c n -> p (c n)")

            def x1T_copy(t, place=lane):
                at_least(act, x1T_ready, t + 1)
                nc.scalar.activation(flat(place.x1T), place.front_bank, ACT.Copy).then_inc(x1T_copied, 1)

            def probs(t, place=lane):
                n = slice(place.n, place.n + 1)
                at_least(act, nmx_ready, t + 1)
                nc.scalar.activation(place.p, place.sc, ACT.Exp, bias=nmx_sb[:, n], accum_out=sum_sb[:, n]
                                     ).then_inc(p_ready, 1)

            def pT_copy(t, place=lane):
                at_least(act, pT_ready, t + 1)
                nc.scalar.activation(place.pT, place.front_bank[:, 0:P], ACT.Copy).then_inc(pT_copied, 1)

            def x2_norm(t, place=lane):
                at_least(act, nmr_ready, t + 1)
                nc.scalar.activation(place.x2, place.bank, ACT.Identity, bias=nmr_sb[:, place.n:place.n + 1],
                                     scale=rstd_sb[:, place.n, 1:2]).then_inc(x2_ready, 1)

            def x2T_copy(t, place=lane):
                at_least(act, x2T_ready, t + 1)
                nc.scalar.activation(flat(place.x2T), place.bank, ACT.Copy).then_inc(x2T_copied, 1)

            def z1_copy(g, b):
                at_least(act, y_added, GU * (g + 1))
                at_least(act, x1_ready, G * g)
                nc.scalar.activation(z1_sb[:, b, :], y_ps[:, b, :], ACT.Copy).then_inc(z1_by_act, 1)

            act.wait_ge(b_stored, G)
            for b in range(G):
                act.wait_ge(dx_ready, b + 1)
                product(0, 0, 0, b, 0)
            act.wait_ge(xd_ready, G)
            act.wait_ge(A_ready, 1)
            act.wait_ge(zeroed, 1)

            def iteration(g, j):
                i = IT * g + j
                tile = finished_tile(g, j)
                last = g == NG - 1 and isinstance(j, int) and j == IT - 1
                if isinstance(j, int) and j == 0:
                    if g == 0:
                        act.wait_ge(delta_ready, G)
                    else:
                        act.wait_ge(delta_stored, loads(G * (g + 1) - 1))
                for u in range(U):
                    k = U * i + u
                    q, c = u // C, u % C
                    at_least(act, h_ready, k - RA + 1)
                    s = Q * j + q
                    A_col = A_sb[:, c, s:s + 1] if isinstance(s, int) else A_sb[:, c, one(s)]
                    nc.scalar.activation(a_sb[:, u % RA, :, 1:], delta_sb[:, g % 2, c, :, 1:], ACT.Exp, scale=A_col
                                         ).then_inc(a_ready, 1)
                    if q < Q - 1:
                        product(g % 2, Q * i + q + 1, q + 1, c, U * (i - 1) + C * (q + 2))
                    elif not last:
                        if c == 0 and has_projection(g):
                            at_least(act, dx_ready, (i + 1) // IT * IT + G)
                            at_least(act, b_stored, (i + 1) // IT * IT + G)
                        half = ((i + 1) // IT) % 2 if isinstance(j, int) else (
                            (g % 2) if not has_projection(g) else (j + 1 + IT * g) // IT % 2)
                        product(half, Q * (i + 1), 0, c, U * i + C)
                    if has_projection(g):
                        if u == ACT_SLOT["copy_lo"]:
                            copy_lo(i + G)
                        if u == ACT_SLOT["sp_abs"]:
                            sp_abs(i + G)
                        if u == ACT_SLOT["sp_exp"]:
                            sp_exp(i + G)
                        if u == ACT_SLOT["sp_ln"]:
                            sp_ln(i + G)
                    if g == 0 and u == ACT_SLOT["F"]:
                        at_least(act, fac_added, (RANK - 1) * (j + 1))
                        nc.scalar.activation(F_sb[:, one(j), :].rearrange("p a d -> p (a d)"), fac_sb[:, 0, :],
                                             ACT.Copy, scale=FSCALE).then_inc(fsum_copied, 1)
                    if tile is not None:
                        if u == ACT_SLOT["probs"]:
                            probs(tile)
                        if u == ACT_SLOT["pT"]:
                            pT_copy(tile)
                        if u == ACT_SLOT["x2_norm"]:
                            x2_norm(tile)
                        if u == ACT_SLOT["x2T"]:
                            x2T_copy(tile)
                    if prepares_x1(g) and u == ACT_SLOT["x1T"]:
                        x1T_copy(i - G)
                    if g > 0 and isinstance(j, int) and j == 0 and u == ACT_SLOT["z1"]:
                        z1_copy(g - 1, 2)
                        z1_copy(g - 1, 3)

            run_iterations(act, iteration)

            probs(*before_last)
            pT_copy(*before_last)
            x2_norm(*before_last)
            x2T_copy(*before_last)
            for t, place in last_tiles:
                x1T_copy(t, place)
            for step in (probs, pT_copy):
                for t, place in last_tiles:
                    step(t, place)
            x2_norm(*last_tiles[0])
            for n, (t, place) in enumerate(last_tiles):
                if n < G - 1:
                    x2_norm(*last_tiles[n + 1])
                x2T_copy(t, place)

        @block.tensor
        def _(pe):
            def transpose(dst, src, start=True):
                return nc.tensor.matmul(dst, src, ident_sb[:, :], start=start, stop=True, is_transpose=True,
                                        skip_group_check=True)

            def proj_bc(t, probs_done):
                at_least(pe, pT_copied, probs_done)
                at_least(pe, xT_loaded, loads(t))
                at_least(pe, dx_ready, t)
                nc.tensor.matmul(pj_ps[:, R:R + 2 * S], ones_sb[:, :], biases_sb[:, D:D + 2 * S], start=True,
                                 stop=False)
                for c in range(C):
                    nc.tensor.matmul(pj_ps[:, R:R + 2 * S], xT_in[:, c, :], WdbcT_sb[:, c, R:R + 2 * S], start=False,
                                     stop=c == C - 1)

            def proj_lo(t):
                for c in range(C):
                    last = nc.tensor.matmul(pj_ps[:, 0:R], WdbcT_sb[:, c, 0:R], xT_in[:, c, :], start=c == 0,
                                            stop=c == C - 1)
                last.then_inc(lo_ready, 1)

            def proj_ct(t):
                at_least(pe, bc_copied, t + 1)
                transpose(pj_ps[0:S, 0:P], bc_sb[:, S:2 * S]).then_inc(ct_ready, 1)

            def proj_z(t, chunks):
                if 0 in chunks:
                    at_least(pe, ct_copied, t + 1)
                    nc.tensor.matmul(pj_ps[:, :], biases_sb[:, D + 2 * S:NB], sel_sb[:, :], start=True, stop=False,
                                     skip_group_check=True)
                for c in chunks:
                    last = nc.tensor.matmul(pj_ps[:, c * P:(c + 1) * P], WdtT_sb[:, c * P:(c + 1) * P], lo_sb[:, :],
                                            start=False, stop=c == C - 1, skip_group_check=True)
                if C - 1 in chunks:
                    last.then_inc(z_ready, 1)

            def proj_dT(t):
                at_least(pe, delta_ready, t + 1)
                for c in range(C):
                    last = transpose(pj_ps[:, c * P:(c + 1) * P], delta_t[:, c, :])
                last.then_inc(dT_ready, 1)

            pe.wait_ge(Wdbc_in, 16)
            def xT_chunk(c):
                return prod_sb[:, 1, :, c * P:(c + 1) * P]

            for c in range(C):
                pe.wait_ge(first_xT_in[c], 16)
                last = nc.tensor.matmul(bx_ps[:, 0, :], WdbcT_sb[:, c, 0:R], xT_chunk(c), start=c == 0, stop=c == C - 1)
            last.then_inc(lo_ready, G)
            for c in range(C):
                last = nc.tensor.matmul(bx_ps[0:2 * S, 1, :], WdbcT_sb[:, c, R:R + 2 * S], xT_chunk(c), start=c == 0,
                                        stop=c == C - 1)
            last.then_inc(ct_ready, G)
            pe.wait_ge(Wdt_in, 16)
            pe.wait_ge(bc_copied, G)
            for b in range(G):
                for c in range(C):
                    nc.tensor.matmul(y_ps[:, b, c * P:(c + 1) * P], WdtT_sb[:, c * P:(c + 1) * P],
                                     first_lo[:, b * P:(b + 1) * P], start=c == 0, stop=False, skip_group_check=True)
                if b == 0:
                    pe.wait_ge(biases_ready, PARTS)
                    pe.wait_ge(sel_ready, 1)
                nc.tensor.matmul(y_ps[:, b, :], biases_sb[:, D + 2 * S:NB], sel_sb[:, :], start=False, stop=True,
                                 skip_group_check=True).then_inc(z_ready, 1)
            pe.wait_ge(ones_ready, 1)
            pe.wait_ge(ident_in, 16)
            pe.wait_ge(ct_copied, G)
            for b in range(G):
                last = nc.tensor.matmul(at_ps[:, b * S:(b + 1) * S], first_bcT[0:S, b * P:(b + 1) * P],
                                        ident_sb[0:S, 0:S], start=True, stop=True, is_transpose=True, skip_group_check=True)
            last.then_inc(BT_ready, 1)
            for b in range(G):
                pe.wait_ge(delta_ready, b + 1)
                for c in range(C):
                    last = transpose(y_ps[:, b, c * P:(c + 1) * P], delta_sb[:, 0, c, b, :])
                last.then_inc(dT_ready, 1)

            def x1_transpose(t, projected, place=lane):
                at_least(pe, x1_ready, t + 1)
                if place is lane:
                    at_least(pe, dx_ready, projected)
                    at_least(pe, pT_copied, t)
                for c in range(C):
                    last = transpose(place.front_bank[:, c * P:(c + 1) * P], place.x1[:, c * P:(c + 1) * P])
                last.then_inc(x1T_ready, 1)

            def scores(t, place=lane):
                at_least(pe, x1T_copied, t + 1)
                if place is lane:
                    at_least(pe, ctxT_loaded, 16 * (t + 1))
                else:
                    pe.wait_ge(last_ctx_in, 32)
                for c in range(C):
                    last = nc.tensor.matmul(place.front_bank[:, 0:P], place.x1T[:, c, :], place.ctxT[:, c, :], start=c == 0,
                                            stop=c == C - 1)
                last.then_inc(scores_ready, 1)

            def p_transpose(t, place=lane):
                at_least(pe, pn_ready, t + 1)
                transpose(place.front_bank[:, 0:P], place.pn).then_inc(pT_ready, 1)

            def residual(t, place=lane):
                at_least(pe, pT_copied, t + 1)
                if place is lane:
                    at_least(pe, o_ready, t)
                for c in range(C):
                    transpose(place.bank[:, c * P:(c + 1) * P], place.x1T[:, c, :], start=c == 0)

            def readout(t, place=lane):
                if place is lane:
                    at_least(pe, ctx_loaded, 16 * (t + 1))
                nc.tensor.matmul(place.bank, place.pT, place.ctx, start=False, stop=True, skip_group_check=True
                                 ).then_inc(z2_ready, 1)

            def x2_transpose(t, place=lane):
                at_least(pe, x2_ready, t + 1)
                for c in range(C):
                    last = transpose(place.bank[:, c * P:(c + 1) * P], place.x2[:, c * P:(c + 1) * P])
                last.then_inc(x2T_ready, 1)

            def ffn(t, c, place=lane):
                if c == 0:
                    pe.wait_ge(F_ready, C)
                    at_least(pe, x2T_copied, t + 1)
                    nc.tensor.matmul(place.bank, ones_sb[:, :], biases_sb[:, 0:D], start=True, stop=False)
                last = nc.tensor.matmul(place.bank, place.x2T[:, c, :], F_sb[:, c, :], start=False,
                                        stop=c == C - 1)
                if c == C - 1:
                    last.then_inc(z3_ready, 1)

            def unit_bx(g, j, u):
                i = IT * g + j
                q, c = u // C, u % C
                if c == 0:
                    at_least(pe, prod_ready, G * (Q * i + q + 1))
                at_least(pe, h_ready, U * i + u - 1)
                for b in range(G):
                    last = transpose(bx_ps[:, u % 2, b * P:(b + 1) * P], prod_sb[:, q, b, c * P:(c + 1) * P])
                last.then_inc(bx_ready, 1)

            def unit_y(k, u):
                at_least(pe, hc_ready, k + 1)
                c = u % C
                for b in range(G):
                    last = transpose(y_ps[:, b, c * P:(c + 1) * P], h_sb[:, u % RH, b * P:(b + 1) * P], start=False)
                last.then_inc(y_added, 1)

            def skip(g):
                at_least(pe, z1_by_dve, 2 * g)
                at_least(pe, z1_by_act, 2 * g)
                at_least(pe, xd_ready, G * (g + 1))
                for b in range(G):
                    for c in range(C):
                        last = transpose(y_ps[:, b, c * P:(c + 1) * P], xd_sb[:, b, c, :], start=c == 0)
                last.then_inc(skip_added, 1)

            def iteration(g, j):
                i = IT * g + j
                tile = finished_tile(g, j)
                for u in range(U):
                    unit_bx(g, j, u)
                    k = U * i + u - LAG
                    turn = isinstance(j, int) and j == 0
                    if turn and u == LAG + TURN:
                        skip(g)
                        for n in range(TURN):
                            unit_y(k - TURN + n, n)
                    if not (isinstance(k, int) and k < 0) and not (turn and LAG <= u < LAG + TURN):
                        unit_y(k, (u - LAG) % U)
                    if has_projection(g):
                        if u == PE_SLOT["bc"]:
                            proj_bc(i + G, 0 if tile is None else tile + 1)
                        if u == PE_SLOT["lo"]:
                            proj_lo(i + G)
                        if u == PE_SLOT["ct"]:
                            proj_ct(i + G)
                        if u == PE_SLOT["z"][0]:
                            proj_z(i + G, range(C // 2))
                        if u == PE_SLOT["z"][1]:
                            proj_z(i + G, range(C // 2, C))
                        if u == PE_SLOT["dT"]:
                            proj_dT(i + G)
                    if tile is not None:
                        if u == PE_SLOT["residual"]:
                            residual(tile)
                        if u == PE_SLOT["readout"]:
                            readout(tile)
                        if u == PE_SLOT["x2T"]:
                            x2_transpose(tile)
                        for c in range(C):
                            if u == PE_SLOT["ffn"][c]:
                                ffn(tile, c)
                    if prepares_x1(g):
                        if u == PE_SLOT["x1T"]:
                            x1_transpose(i - G, i + G + 1 if has_projection(g) else NT)
                        if u == PE_SLOT["scores"]:
                            scores(i - G)
                        if u == PE_SLOT["pT"]:
                            p_transpose(i - G)

            run_iterations(pe, iteration)
            for u in range(U - LAG, U):
                if u == U - 2:
                    residual(*before_last)
                    readout(*before_last)
                unit_y(GU * NG - U + u, u)
            x2_transpose(*before_last)
            ffn(NT - G - 1, 0)
            ffn(NT - G - 1, 1)
            x1_transpose(NT - G, NT, last_lanes[0])
            ffn(NT - G - 1, 2)
            for n, (t, place) in enumerate(last_tiles):
                if n < G - 1:
                    x1_transpose(t + 1, NT, last_lanes[n + 1])
                scores(t, place)
            ffn(NT - G - 1, 3)
            for t, place in last_tiles:
                p_transpose(t, place)
            for t, place in last_tiles:
                residual(t, place)
                readout(t, place)
            x2_transpose(*last_tiles[0])
            for n, (t, place) in enumerate(last_tiles):
                if n < G - 1:
                    x2_transpose(*last_tiles[n + 1])
                for c in range(C):
                    ffn(t, c, place)

        @block.vector
        def _(dve):
            nc.vector.memset(a_sb[:, :, :, 0:1], 0.0).then_inc(zeroed, 1)
            dve.wait_ge(biases_in, 16)
            for part in range(PARTS):
                rest = raw_sb if part == 0 else rest_sb
                nc.vector.tensor_copy(part_sb[:, :], rest[:, :]).then_inc(bias_step, 1)
                dve.wait_ge(bias_step, 2 * part + 1)
                rows = slice(32 * part, 32 * part + 32)
                nc.vector.tensor_copy(biases_sb[rows, :], part_sb[rows, :]).then_inc(biases_ready, 1)
                if part < PARTS - 1:
                    nc.vector.tensor_tensor(rest_sb[:, :], rest[:, :], part_sb[:, :], ALU.subtract
                                            ).then_inc(bias_step, 1)
                    dve.wait_ge(bias_step, 2 * part + 2)
                    dve.wait_ge(biases_ready, part + 1)
            dve.wait_ge(sel_in, 16)
            nc.vector.tensor_copy(sel_sb[:, :], sel_raw[:, :]).then_inc(sel_ready, 1)
            dve.wait_ge(Dv_in, 16)
            nc.vector.tensor_scalar(D1_sb[:, :], D1_sb[:, :], 1.0, None, ALU.add).then_inc(D1_ready, 1)

            def expand_mask():
                dve.wait_ge(mask_in, 16)
                nc.vector.tensor_scalar(neg_sb[:, :], mask_sb[:, :], BIG, BIG, ALU.mult, ALU.subtract
                                        ).then_inc(neg_ready, 1)
                dve.wait_ge(neg_ready, 1)
                nc.vector.reduce_max(best_sb[:, :], neg_sb[:, :].rearrange("p (b n) -> p b n", n=P), AX_X
                                     ).then_inc(best_ready, 1)
                dve.wait_ge(best_ready, 1)
                nc.vector.tensor_scalar(valid_sb[:, :], best_sb[:, :], 0.0, None, ALU.is_ge).then_inc(valid_ready, 1)
                dve.wait_ge(valid_ready, 1)

            def copy_ct(t):
                at_least(dve, ct_ready, t + 1)
                at_least(dve, ct_stored, loads(t))
                nc.vector.tensor_copy(ct_sb[:, :], pj_ps[0:S, 0:P]).then_inc(ct_copied, 1)

            def softplus_end(t):
                at_least(dve, spln_done, t + 1)
                at_least(dve, delta_stored, loads(t - 1))
                nc.vector.scalar_tensor_tensor(delta_t[:, :, :].rearrange("p c n -> p (c n)"), pj_ps[:, :], 0.0,
                                               sp_sb[:, :], ALU.max, ALU.add).then_inc(delta_ready, 1)

            def delta_x(g, tile, t):
                at_least(dve, dT_ready, t + 1)
                at_least(dve, x_loaded, loads(t))
                at_least(dve, prod_ready, G * S * (g - 1))
                nc.vector.tensor_tensor(dx_sb[:, g % 2, one(tile), :].rearrange("p a d -> p (a d)"), pj_ps[:, :],
                                        x_in[:, :], ALU.mult).then_inc(dx_ready, 1)

            dve.wait_ge(ct_ready, G)
            dve.wait_ge(bbc_in, 16)
            nc.vector.tensor_scalar(first_bcT, bx_ps[0:2 * S, 1, :], bbc_sb[:, :], None, ALU.add).then_inc(ct_copied, G)
            dve.wait_ge(A_exp, 1)
            nc.vector.tensor_scalar(A_sb[:, :, :], A_sb[:, :, :], -1.0, None, ALU.mult).then_inc(A_ready, 1)
            dve.wait_ge(BT_ready, 1)
            nc.vector.tensor_copy(B_sb[:, 0, :, :], at_ps[:, 0:G * S].rearrange("p (b s) -> p s b", s=S)
                                  ).then_inc(b_stored, G)
            for b in range(G):
                dve.wait_ge(spln_done, b + 1)
                nc.vector.scalar_tensor_tensor(delta_sb[:, 0, :, b, :], y_ps[:, b, :].rearrange("p (c n) -> p c n", n=P),
                                               0.0, first_sp(b).rearrange("p (c n) -> p c n", n=P), ALU.max, ALU.add
                                               ).then_inc(delta_ready, 1)
            dve.wait_ge(first_x_in, 16)
            for b in range(G):
                dve.wait_ge(dT_ready, b + 1)
                nc.vector.tensor_tensor(dx_sb[:, 0, b, :], y_ps[:, b, :], first_x(b), ALU.mult).then_inc(dx_ready, 1)

            def stats(n, tiles):
                for t, column, src in tiles:
                    nc.vector.bn_stats(st_sb[:, column, n, :], src).then_inc(st_done[n], 1)

            def means(n, tiles):
                for t, column in tiles:
                    at_least_alone(dve, st_done[n], t + 1)
                    nc.vector.bn_aggr(mv_sb[:, column, n, :], st_sb[:, column, n, :]).then_inc(mv_done[n], 1)
                for t, column in tiles:
                    at_least(dve, mv_done[n], t + 1)
                    nc.vector.tensor_scalar(ve_sb[:, column, n:n + 1], mv_sb[:, column, n, 1:2], EPS, None, ALU.add
                                            ).then_inc(ve_done[n], 1)

            def z1_stats(t, place):
                stats(0, [(t, 0, z1_sb[:, one(place), :].rearrange("p a d -> p (a d)"))])

            def x1_norm(t, z1, place):
                at_least(dve, rstd_done[0], t + 1)
                nc.vector.tensor_scalar(place.x1, z1, mv_sb[:, place.n, 0, 0:1], rstd_sb[:, place.n, 0:1],
                                        ALU.subtract, ALU.mult).then_inc(x1_ready, 1)

            def mask_and_max(t, place=lane):
                n = slice(place.n, place.n + 1)
                at_least(dve, scores_ready, t + 1)
                neg = neg_sb[:, t * P:(t + 1) * P] if isinstance(t, int) else neg_sb[:, bass.ds(t * P, P)]
                nc.vector.scalar_tensor_tensor(place.sc, place.front_bank[:, 0:P], SCALE, neg, ALU.mult, ALU.add
                                               ).then_inc(masked, 1)
                at_least(dve, masked, t + 1)
                nc.vector.reduce_max(mx_sb[:, n], place.sc, AX_X).then_inc(max_done, 1)
                at_least(dve, max_done, t + 1)
                nc.vector.tensor_scalar(nmx_sb[:, n], mx_sb[:, n], -1.0, None, ALU.mult).then_inc(nmx_ready, 1)

            def normalise_probs(t, place=lane):
                n = slice(place.n, place.n + 1)
                at_least(dve, p_ready, t + 1)
                nc.vector.reciprocal(rs_sb[:, n], sum_sb[:, n]).then_inc(rs_done, 1)
                at_least(dve, rs_done, t + 1)
                nc.vector.tensor_tensor(rv_sb[:, n], rs_sb[:, n], valid_sb[:, one(t)], ALU.mult).then_inc(rv_done, 1)
                at_least(dve, rv_done, t + 1)
                nc.vector.tensor_scalar(place.pn, place.p, rv_sb[:, n], None, ALU.mult).then_inc(pn_ready, 1)

            def z2_stats(t, place=lane):
                at_least(dve, z2_ready, t + 1)
                stats(1, [(t, place.n, place.bank)])

            def z2_shift(t, place=lane):
                at_least(dve, rstd_done[1], t + 1)
                nc.vector.scalar_tensor_tensor(nmr_sb[:, place.n:place.n + 1], mv_sb[:, place.n, 1, 0:1], -1.0,
                                               rstd_sb[:, place.n, 1:2], ALU.mult, ALU.mult).then_inc(nmr_ready, 1)

            def z3_stats(t, place=lane):
                at_least(dve, z3_ready, t + 1)
                stats(2, [(t, place.n, place.bank)])

            def z3_norm(t, place=lane):
                at_least(dve, rstd_done[2], t + 1)
                if place is lane:
                    at_least(dve, out_stored, 16 * t)
                nc.vector.tensor_scalar(place.o, place.bank, mv_sb[:, place.n, 2, 0:1], rstd_sb[:, place.n, 2:3],
                                        ALU.subtract, ALU.mult).then_inc(o_ready, 1)

            def z1_copy(g, b):
                at_least(dve, y_added, GU * (g + 1))
                at_least(dve, x1_ready, G * g)
                nc.vector.tensor_copy(z1_sb[:, b, :], y_ps[:, b, :]).then_inc(z1_by_dve, 1)

            pairs = [(r, r + n) for n in (4, 2, 1) for r in range(n)]

            def add_factor(j, step):
                r, other = pairs[step]
                if step == 0:
                    at_least(dve, fac_loaded, 16 * (j + 1))
                if step >= RANK // 2:
                    at_least(dve, fac_added, (RANK - 1) * j + step)
                nc.vector.tensor_tensor(fac_sb[:, r, :], fac_sb[:, r, :], fac_sb[:, other, :], ALU.add
                                        ).then_inc(fac_added, 1)

            def iteration(g, j):
                i = IT * g + j
                tile = finished_tile(g, j)
                for u in range(U):
                    k = U * i + u
                    at_least(dve, a_ready, k + 1)
                    at_least(dve, bx_ready, k + 1)
                    at_least(dve, y_added, k - RH + 1)
                    nc.vector.tensor_tensor_scan(h_sb[:, u % RH, :], a_sb[:, u % RA, :, :].rearrange("p b n -> p (b n)"),
                                                 bx_ps[:, u % 2, :], 0.0, ALU.mult, ALU.add).then_inc(h_ready, 1)
                    if g == 0 and isinstance(j, int) and u == LAG:
                        expand_mask()
                    if g == 0 and FACTOR_SLOT <= u < FACTOR_SLOT + RANK - 1:
                        add_factor(j, u - FACTOR_SLOT)
                    if has_projection(g):
                        if u == DVE_SLOT["copy_ct"]:
                            copy_ct(i + G)
                        if u == DVE_SLOT["softplus_end"]:
                            softplus_end(i + G)
                        if u == DVE_SLOT["delta_x"]:
                            delta_x(g + 1, j, i + G)
                    if tile is not None:
                        if u == DVE_SLOT["z2_stats"]:
                            z2_stats(tile)
                        if u == DVE_SLOT["z2_mean"]:
                            means(1, [(tile, 0)])
                        if u == DVE_SLOT["z2_shift"]:
                            z2_shift(tile)
                        if u == DVE_SLOT["z3_stats"]:
                            z3_stats(tile)
                        if u == DVE_SLOT["z3_mean"]:
                            means(2, [(tile, 0)])
                        if u == DVE_SLOT["z3_norm"]:
                            z3_norm(tile)
                    if prepares_x1(g):
                        if u == DVE_SLOT["z1_stats"]:
                            if isinstance(j, int) and j == 0:
                                dve.wait_ge(z1_by_act, 2 * g)
                                dve.wait_ge(z1_by_dve, 2 * g)
                            z1_stats(i - G, j)
                        if u == DVE_SLOT["z1_mean"]:
                            means(0, [(i - G, 0)])
                        if u == DVE_SLOT["x1_norm"]:
                            x1_norm(i - G, z1_sb[:, one(j), :].rearrange("p a d -> p (a d)"), lane)
                        if u == DVE_SLOT["mask"]:
                            mask_and_max(i - G)
                        if u == DVE_SLOT["normalise"]:
                            normalise_probs(i - G)
                    if g > 0 and isinstance(j, int) and j == 0 and u == LAG - 1:
                        z1_copy(g - 1, 0)
                        z1_copy(g - 1, 1)

            run_iterations(dve, iteration)

            z2_stats(*before_last)
            means(1, [(NT - G - 1, 0)])
            z2_shift(*before_last)
            dve.wait_ge(y_added, GU * NG)
            stats(0, [(t, place.n, place.bank) for t, place in last_tiles])
            means(0, [(t, place.n) for t, place in last_tiles])
            for t, place in last_tiles:
                x1_norm(t, place.bank, place)
            mask_and_max(*last_tiles[0])
            for n, (t, place) in enumerate(last_tiles):
                if n < G - 1:
                    mask_and_max(*last_tiles[n + 1])
                normalise_probs(t, place)
            z3_stats(*before_last)
            means(2, [(NT - G - 1, 0)])
            for t, place in last_tiles:
                z2_stats(t, place)
                means(1, [(t, place.n)])
                if place is last_lanes[0]:
                    z3_norm(*before_last)
                else:
                    z2_shift(t - 1, last_lanes[place.n - 2])
            z2_shift(*last_tiles[-1])
            for t, place in last_tiles:
                z3_stats(t, place)
                means(2, [(t, place.n)])
                z3_norm(t, place)


def kernel(x, ctx_2048, mask_BxS2_bk0, L0_attn_W_dbc, L0_attn_b_dbc, L0_attn_W_dt, L0_attn_b_dt, L0_attn_A_log,
           L0_attn_D, L0_ffn_factors, L0_ffn_bias):
    import numpy as np
    import concourse.bacc as bacc
    from concourse import mybir as mb
    from concourse.bass_utils import run_bass_kernel_spmd

    def channels_first(v):
        v = np.asarray(v).transpose(0, 2, 1).reshape(NT, C, P, P)
        return np.ascontiguousarray(v.transpose(0, 2, 1, 3))

    def quadrants(*blocks):
        rows = np.zeros((KB, sum(v.shape[1] for v in blocks)), np.float32)
        for first in range(0, KB, 32):
            column = 0
            for v in blocks:
                rows[first:first + v.shape[0], column:column + v.shape[1]] = v
                column += v.shape[1]
        return rows

    b_dbc = np.asarray(L0_attn_b_dbc)
    arrays = {
        "x": np.asarray(x),
        "xT": channels_first(x),
        "ctx": np.asarray(ctx_2048),
        "ctxT": channels_first(ctx_2048),
        "mask": np.asarray(mask_BxS2_bk0).reshape(1, NT * P),
        "WdbcT": np.ascontiguousarray(np.asarray(L0_attn_W_dbc).T),
        "b_lo": np.ascontiguousarray(b_dbc[:R].reshape(P, 1)),
        "b_bc": np.ascontiguousarray(b_dbc[R:].reshape(2 * S, 1)),
        "bias_rows": quadrants(np.concatenate([np.asarray(L0_ffn_bias), b_dbc[R:]]).reshape(1, D + 2 * S),
                               np.asarray(L0_attn_b_dt).reshape(C, P)),
        "WdtT": np.ascontiguousarray(np.asarray(L0_attn_W_dt).T),
        "A_log": np.asarray(L0_attn_A_log),
        "Dv": np.ascontiguousarray(np.asarray(L0_attn_D).reshape(C, P).T),
        "factors": np.asarray(L0_ffn_factors),
        "ident": np.eye(P, dtype=np.float32),
        "sel_rows": quadrants(np.repeat(np.eye(C, dtype=np.float32), P, axis=1)),
    }
    nc = bacc.Bacc("TRN2", target_bir_lowering=False, num_devices=1)
    args = {n: nc.dram_tensor(f"in_{n}", v.shape, mb.dt.from_np(v.dtype), kind="ExternalInput").ap()
            for n, v in arrays.items()}
    cT = nc.dram_tensor("c_spread", (NG, S, G, P), F32, kind="Internal").ap()
    out = nc.dram_tensor("out", (NT, P, D), F32, kind="ExternalOutput").ap()
    decoder_layer(nc, cT=cT, out=out, **args)
    r = run_bass_kernel_spmd(nc, [{f"in_{n}": v for n, v in arrays.items()}], core_ids=[0])
    return r.results[0]["out"]
```
